# Optimizing a Trainium2 kernel written in Bass

```python
import numpy as np
import jax
import jax.numpy as jnp

def _softmax(x, axis=-1):
    return jax.nn.softmax(x, axis=axis)

def _gelu(x):
    return jax.nn.gelu(x, approximate=True)

def _silu(x):
    return jax.nn.silu(x)

def _sigmoid(x):
    return jax.nn.sigmoid(x)

def _layernorm(x, axis=-1, eps=1e-05):
    m = jnp.mean(x, axis=axis, keepdims=True)
    v = jnp.var(x, axis=axis, keepdims=True)
    return (x - m) / jnp.sqrt(v + eps)

def _scatter_add(tgt, idx, src, axis=0):
    return tgt.at[idx].add(src)

def _segment_sum(src, seg, n):
    return jax.ops.segment_sum(src, seg, n)
kernel_name = 'mk_dlrm_tower_d1_rec_r8_60fe41'

def setup_inputs(seed: int=0):
    np.random.seed(seed)
    _w = jnp.asarray

    def _rec_inputs():
        import jax
        import jax.numpy as jnp
        _tk = jax.random.key(seed)
        dense_ctx = jax.random.normal(jax.random.fold_in(_tk, 190), (512, 16), jnp.float32)
        ids = jnp.stack([jax.random.randint(jax.random.fold_in(_tk, 200 + f), (512,), 0, v, jnp.int32) for f, v in enumerate([12500, 12500, 12500, 125000, 1000, 12500, 1250, 1000, 1250, 1250, 12500, 1000, 1250, 125000, 125000, 1000, 1000, 12500, 12500, 1000, 12500, 1000, 1250, 1000, 1250, 1250, 1250, 1000, 1000, 1250, 1000, 1000])], axis=1)
        tbl_0 = 0.05 * jax.random.normal(jax.random.fold_in(_tk, 500 + 0), (12500, 64), jnp.float32)
        tbl_1 = 0.05 * jax.random.normal(jax.random.fold_in(_tk, 500 + 1), (12500, 64), jnp.float32)
        tbl_2 = 0.05 * jax.random.normal(jax.random.fold_in(_tk, 500 + 2), (12500, 64), jnp.float32)
        tbl_3 = 0.05 * jax.random.normal(jax.random.fold_in(_tk, 500 + 3), (125000, 64), jnp.float32)
        tbl_4 = 0.05 * jax.random.normal(jax.random.fold_in(_tk, 500 + 4), (1000, 64), jnp.float32)
        tbl_5 = 0.05 * jax.random.normal(jax.random.fold_in(_tk, 500 + 5), (12500, 64), jnp.float32)
        tbl_6 = 0.05 * jax.random.normal(jax.random.fold_in(_tk, 500 + 6), (1250, 64), jnp.float32)
        tbl_7 = 0.05 * jax.random.normal(jax.random.fold_in(_tk, 500 + 7), (1000, 64), jnp.float32)
        tbl_8 = 0.05 * jax.random.normal(jax.random.fold_in(_tk, 500 + 8), (1250, 64), jnp.float32)
        tbl_9 = 0.05 * jax.random.normal(jax.random.fold_in(_tk, 500 + 9), (1250, 64), jnp.float32)
        tbl_10 = 0.05 * jax.random.normal(jax.random.fold_in(_tk, 500 + 10), (12500, 64), jnp.float32)
        tbl_11 = 0.05 * jax.random.normal(jax.random.fold_in(_tk, 500 + 11), (1000, 64), jnp.float32)
        tbl_12 = 0.05 * jax.random.normal(jax.random.fold_in(_tk, 500 + 12), (1250, 64), jnp.float32)
        tbl_13 = 0.05 * jax.random.normal(jax.random.fold_in(_tk, 500 + 13), (125000, 64), jnp.float32)
        tbl_14 = 0.05 * jax.random.normal(jax.random.fold_in(_tk, 500 + 14), (125000, 64), jnp.float32)
        tbl_15 = 0.05 * jax.random.normal(jax.random.fold_in(_tk, 500 + 15), (1000, 64), jnp.float32)
        tbl_16 = 0.05 * jax.random.normal(jax.random.fold_in(_tk, 500 + 16), (1000, 64), jnp.float32)
        tbl_17 = 0.05 * jax.random.normal(jax.random.fold_in(_tk, 500 + 17), (12500, 64), jnp.float32)
        tbl_18 = 0.05 * jax.random.normal(jax.random.fold_in(_tk, 500 + 18), (12500, 64), jnp.float32)
        tbl_19 = 0.05 * jax.random.normal(jax.random.fold_in(_tk, 500 + 19), (1000, 64), jnp.float32)
        tbl_20 = 0.05 * jax.random.normal(jax.random.fold_in(_tk, 500 + 20), (12500, 64), jnp.float32)
        tbl_21 = 0.05 * jax.random.normal(jax.random.fold_in(_tk, 500 + 21), (1000, 64), jnp.float32)
        tbl_22 = 0.05 * jax.random.normal(jax.random.fold_in(_tk, 500 + 22), (1250, 64), jnp.float32)
        tbl_23 = 0.05 * jax.random.normal(jax.random.fold_in(_tk, 500 + 23), (1000, 64), jnp.float32)
        tbl_24 = 0.05 * jax.random.normal(jax.random.fold_in(_tk, 500 + 24), (1250, 64), jnp.float32)
        tbl_25 = 0.05 * jax.random.normal(jax.random.fold_in(_tk, 500 + 25), (1250, 64), jnp.float32)
        tbl_26 = 0.05 * jax.random.normal(jax.random.fold_in(_tk, 500 + 26), (1250, 64), jnp.float32)
        tbl_27 = 0.05 * jax.random.normal(jax.random.fold_in(_tk, 500 + 27), (1000, 64), jnp.float32)
        tbl_28 = 0.05 * jax.random.normal(jax.random.fold_in(_tk, 500 + 28), (1000, 64), jnp.float32)
        tbl_29 = 0.05 * jax.random.normal(jax.random.fold_in(_tk, 500 + 29), (1250, 64), jnp.float32)
        tbl_30 = 0.05 * jax.random.normal(jax.random.fold_in(_tk, 500 + 30), (1000, 64), jnp.float32)
        tbl_31 = 0.05 * jax.random.normal(jax.random.fold_in(_tk, 500 + 31), (1000, 64), jnp.float32)
        _rk = jax.random.fold_in(_tk, 7)
        W_top1 = 0.0606339 * jax.random.normal(jax.random.fold_in(_tk, 801), (272, 512), jnp.float32)
        W_top2 = 0.0441942 * jax.random.normal(jax.random.fold_in(_tk, 802), (512, 256), jnp.float32)
        W_top3 = 0.0625 * jax.random.normal(jax.random.fold_in(_tk, 803), (256, 1), jnp.float32)
        b_top1 = jnp.zeros((512,), jnp.float32)
        b_top2 = jnp.zeros((256,), jnp.float32)
        return (dense_ctx, ids, tbl_0, tbl_1, tbl_2, tbl_3, tbl_4, tbl_5, tbl_6, tbl_7, tbl_8, tbl_9, tbl_10, tbl_11, tbl_12, tbl_13, tbl_14, tbl_15, tbl_16, tbl_17, tbl_18, tbl_19, tbl_20, tbl_21, tbl_22, tbl_23, tbl_24, tbl_25, tbl_26, tbl_27, tbl_28, tbl_29, tbl_30, tbl_31, W_top1, b_top1, W_top2, b_top2, W_top3)
    dense_ctx, ids, tbl_0, tbl_1, tbl_2, tbl_3, tbl_4, tbl_5, tbl_6, tbl_7, tbl_8, tbl_9, tbl_10, tbl_11, tbl_12, tbl_13, tbl_14, tbl_15, tbl_16, tbl_17, tbl_18, tbl_19, tbl_20, tbl_21, tbl_22, tbl_23, tbl_24, tbl_25, tbl_26, tbl_27, tbl_28, tbl_29, tbl_30, tbl_31, W_top1, b_top1, W_top2, b_top2, W_top3 = _rec_inputs()

    def _L0_rec_setup():
        import jax, jax.numpy as jnp
        import numpy as np
        EMB_DIM = 64
        NUM_FIELDS = 32
        NUM_PAIRS = NUM_FIELDS * (NUM_FIELDS - 1) // 2
        D1 = 256
        BATCH = 256
        key = jax.random.key(seed)
        k1, k2, k3 = jax.random.split(key, 3)
        feat_emb = jax.random.normal(k1, (BATCH, NUM_FIELDS, EMB_DIM), dtype=jnp.float32)
        lim_k = float(np.sqrt(6.0 / (EMB_DIM + EMB_DIM)))
        kernel = jax.random.uniform(k2, (EMB_DIM, NUM_PAIRS, EMB_DIM), minval=-lim_k, maxval=lim_k, dtype=jnp.float32)
        lim_w = float(np.sqrt(6.0 / (NUM_PAIRS + D1)))
        W = jax.random.uniform(k3, (D1, NUM_PAIRS), minval=-lim_w, maxval=lim_w, dtype=jnp.float32)
        b = jnp.zeros((D1,), dtype=jnp.float32)
        return {'feat_emb': feat_emb, 'kernel': kernel, 'W': W, 'b': b}
    _L0_rec_all = _L0_rec_setup()
    _L0_rec_in = {k: v for k, v in _L0_rec_all.items() if k in ('kernel', 'W', 'b')}
    del _L0_rec_all
    return {'dense_ctx': dense_ctx, 'ids': ids, 'tbl_0': tbl_0, 'tbl_1': tbl_1, 'tbl_2': tbl_2, 'tbl_3': tbl_3, 'tbl_4': tbl_4, 'tbl_5': tbl_5, 'tbl_6': tbl_6, 'tbl_7': tbl_7, 'tbl_8': tbl_8, 'tbl_9': tbl_9, 'tbl_10': tbl_10, 'tbl_11': tbl_11, 'tbl_12': tbl_12, 'tbl_13': tbl_13, 'tbl_14': tbl_14, 'tbl_15': tbl_15, 'tbl_16': tbl_16, 'tbl_17': tbl_17, 'tbl_18': tbl_18, 'tbl_19': tbl_19, 'tbl_20': tbl_20, 'tbl_21': tbl_21, 'tbl_22': tbl_22, 'tbl_23': tbl_23, 'tbl_24': tbl_24, 'tbl_25': tbl_25, 'tbl_26': tbl_26, 'tbl_27': tbl_27, 'tbl_28': tbl_28, 'tbl_29': tbl_29, 'tbl_30': tbl_30, 'tbl_31': tbl_31, 'W_top1': W_top1, 'b_top1': b_top1, 'W_top2': W_top2, 'b_top2': b_top2, 'W_top3': W_top3, 'L0_rec_kernel': _L0_rec_in['kernel'], 'L0_rec_W': _L0_rec_in['W'], 'L0_rec_b': _L0_rec_in['b']}

def reference(dense_ctx, ids, tbl_0, tbl_1, tbl_2, tbl_3, tbl_4, tbl_5, tbl_6, tbl_7, tbl_8, tbl_9, tbl_10, tbl_11, tbl_12, tbl_13, tbl_14, tbl_15, tbl_16, tbl_17, tbl_18, tbl_19, tbl_20, tbl_21, tbl_22, tbl_23, tbl_24, tbl_25, tbl_26, tbl_27, tbl_28, tbl_29, tbl_30, tbl_31, W_top1, b_top1, W_top2, b_top2, W_top3, L0_rec_kernel, L0_rec_W, L0_rec_b):
    import jax
    import jax.numpy as jnp

    def _L0_rec_ref(feat_emb, kernel, W, b):
        import jax, jax.numpy as jnp
        import numpy as np
        EMB_DIM = 64
        NUM_FIELDS = 32
        NUM_PAIRS = NUM_FIELDS * (NUM_FIELDS - 1) // 2
        D1 = 256
        BATCH = 256
        num_fields = feat_emb.shape[1]
        rows, cols = np.triu_indices(num_fields, k=1)
        p = feat_emb[:, rows, :]
        q = feat_emb[:, cols, :]
        pij = jnp.einsum('bpe,dpe,bpd->bp', p, kernel, q)
        return pij @ W.T + b
    e = jnp.stack([tbl_0[ids[:, 0]], tbl_1[ids[:, 1]], tbl_2[ids[:, 2]], tbl_3[ids[:, 3]], tbl_4[ids[:, 4]], tbl_5[ids[:, 5]], tbl_6[ids[:, 6]], tbl_7[ids[:, 7]], tbl_8[ids[:, 8]], tbl_9[ids[:, 9]], tbl_10[ids[:, 10]], tbl_11[ids[:, 11]], tbl_12[ids[:, 12]], tbl_13[ids[:, 13]], tbl_14[ids[:, 14]], tbl_15[ids[:, 15]], tbl_16[ids[:, 16]], tbl_17[ids[:, 17]], tbl_18[ids[:, 18]], tbl_19[ids[:, 19]], tbl_20[ids[:, 20]], tbl_21[ids[:, 21]], tbl_22[ids[:, 22]], tbl_23[ids[:, 23]], tbl_24[ids[:, 24]], tbl_25[ids[:, 25]], tbl_26[ids[:, 26]], tbl_27[ids[:, 27]], tbl_28[ids[:, 28]], tbl_29[ids[:, 29]], tbl_30[ids[:, 30]], tbl_31[ids[:, 31]]], axis=1)
    z = _L0_rec_ref(e, L0_rec_kernel, L0_rec_W, L0_rec_b)
    z = z.reshape(z.shape[0], -1)
    h = jnp.concatenate([z, dense_ctx], axis=1)
    h = jnp.maximum(h @ W_top1 + b_top1, 0.0)
    h = jnp.maximum(h @ W_top2 + b_top2, 0.0)
    y = h @ W_top3
    return y

_drawn_inputs = setup_inputs


def setup_inputs(seed=0):
    import zlib

    import numpy as np

    out = dict(_drawn_inputs(seed))
    spreads = {'b_top1': (0.0, 0.1), 'b_top2': (0.0, 0.1), 'L0_rec_b': (0.0, 0.1)}
    factors = {'tbl_0': 3.303,
     'tbl_1': 3.068,
     'tbl_2': 3.264,
     'tbl_3': 3.445,
     'tbl_4': 3.634,
     'tbl_5': 3.196,
     'tbl_6': 3.033,
     'tbl_7': 3.08,
     'tbl_8': 3.29,
     'tbl_9': 2.954,
     'tbl_10': 3.424,
     'tbl_11': 3.242,
     'tbl_12': 3.258,
     'tbl_13': 3.309,
     'tbl_14': 3.125,
     'tbl_15': 3.443,
     'tbl_16': 3.553,
     'tbl_17': 3.222,
     'tbl_18': 3.258,
     'tbl_19': 2.949,
     'tbl_20': 3.085,
     'tbl_21': 3.588,
     'tbl_22': 3.633,
     'tbl_23': 3.117,
     'tbl_24': 3.357,
     'tbl_25': 3.181,
     'tbl_26': 3.339,
     'tbl_27': 3.3,
     'tbl_28': 3.416,
     'tbl_29': 3.548,
     'tbl_30': 3.248,
     'tbl_31': 3.337}
    for name, (base, spread) in spreads.items():
        noise = np.random.default_rng([zlib.crc32(name.encode()), seed]).standard_normal(out[name].shape)
        drawn = base * np.exp(spread * noise) if base else spread * noise
        out[name] = jnp.asarray(drawn.astype(out[name].dtype))
    for name, factor in factors.items():
        out[name] = (out[name] * factor).astype(out[name].dtype)
    return out
```

```python
from contextlib import ExitStack

import concourse.bass as bass
from concourse import mybir

FIELDS, DIM = 32, 64
PAIRS = FIELDS * (FIELDS - 1) // 2
PAIR_SPLIT = 4
PBLOCK = PAIRS // PAIR_SPLIT
BATCH, ROWS = 512, 128
TILES = BATCH // ROWS
STEPS = TILES // 2
D1, CTX, H1, H2 = 256, 16, 512, 256
KCHUNK = 32 * DIM


def first_column(j):
    return (j // 2) * (j // 2 - 1) * DIM if j % 2 == 0 else (j // 2) ** 2 * DIM


KCOLS = first_column(FIELDS + 1)
KCHUNKS = KCOLS // KCHUNK


def cut_units():
    units = []
    for j in range(1, FIELDS):
        cuts = [(0, j)] if j <= 24 else [(0, (j + 1) // 2), ((j + 1) // 2, j - (j + 1) // 2)]
        units += [(j, i, n, max(1, round(n * 0.2))) for i, n in cuts]
    return units


UNITS_OF = cut_units()
UNITS = len(UNITS_OF)
SEED = 2 * UNITS
DVE_SUMS = UNITS - 1
PRODUCT_BUFFERS = 4
TAIL_STAGES = 5
TAIL_AFTER = (14, 18, 22, 26, 30)


def starts_pair(u):
    j, i0, *_ = UNITS_OF[u]
    return i0 == 0 and j == max(1, j // 2 * 2)


def last_unit(pair):
    return max(u for u, (j, *_) in enumerate(UNITS_OF) if j // 2 <= pair)


def build(nc, tables, ids, k_cols, w_pairs, b_pairs, ctx_t, w1, b1, w2, b2, w3, y):
    f32, i32 = mybir.dt.float32, mybir.dt.int32
    ALU, ACT, AX = mybir.AluOpType, mybir.ActivationFunctionType, mybir.AxisListType

    ctx = ExitStack()
    with ctx:
        def sb(name, shape, dt=f32):
            return ctx.enter_context(nc.sbuf_tensor(name, shape, dt))

        def sem(name):
            return ctx.enter_context(nc.semaphore(name))

        k_sb = sb("k_sb", [128, KCOLS])
        rows_id = [sb(f"rows_id{h}", [ROWS, FIELDS], i32) for h in range(2)]
        emb = [sb(f"emb{h}", [ROWS, FIELDS * DIM]) for h in range(2)]
        emb_t = [[sb(f"emb_t{s}{p}", [128, ROWS]) for p in range(2)] for s in range(2)]
        product = [sb(f"product{g}", [ROWS, 24, DIM]) for g in range(PRODUCT_BUFFERS)]
        pij = [sb(f"pij{h}", [ROWS, PAIRS]) for h in range(2)]
        pij_t = sb("pij_t", [PBLOCK, PAIR_SPLIT, ROWS])
        z_t = sb("z_t", [128, D1 // 128, ROWS])
        h1_t = sb("h1_t", [128, H1 // 128, ROWS])
        h2_t = sb("h2_t", [128, H2 // 128, ROWS])
        y_row = sb("y_row", [1, BATCH])
        ident = sb("ident", [128, 128])
        w_pairs_sb = sb("w_pairs_sb", [PBLOCK, PAIR_SPLIT, D1])
        b_pairs_sb = sb("b_pairs_sb", [128, D1 // 128])
        ctx_sb = [sb(f"ctx_sb{h}", [CTX, ROWS]) for h in range(2)]
        w1z_sb = sb("w1z_sb", [128, D1 // 128, H1])
        w1c_sb = sb("w1c_sb", [CTX, H1])
        b1_sb = sb("b1_sb", [128, H1 // 128])
        w2_sb = sb("w2_sb", [128, H1 // 128, H2])
        b2_sb = sb("b2_sb", [128, H2 // 128])
        w3_sb = sb("w3_sb", [128, H2 // 128])

        t_ps = [ctx.enter_context(nc.psum_tensor(f"t_ps{p}", [ROWS, 24, DIM], f32)) for p in range(2)]
        emb_ps = ctx.enter_context(nc.psum_tensor("emb_ps", [128, 512], f32))
        tail_ps = ctx.enter_context(nc.psum_tensor("tail_ps", [128, 512], f32))

        ids_loaded = [sem(f"ids_loaded{h}") for h in range(2)]
        ctx_loaded = [sem(f"ctx_loaded{h}") for h in range(2)]
        gathered = [[sem(f"gathered{h}_{m}") for m in range(FIELDS // 2)] for h in range(2)]
        k_loaded = [sem(f"k_loaded{c}") for c in range(KCHUNKS)]
        weights_loaded = sem("weights_loaded")
        zeroed = sem("zeroed")
        ident_ready = sem("ident_ready")
        emb_in_psum = sem("emb_in_psum")
        emb_t_ready = sem("emb_t_ready")
        t_ready = sem("t_ready")
        product_ready = sem("product_ready")
        act_summed = sem("act_summed")
        dve_summed = sem("dve_summed")
        tail_mm = sem("tail_mm")
        tail_out = sem("tail_out")
        y_stored = sem("y_stored")
        gathers_begun = sem("gathers_begun")
        context_free = sem("context_free")

        WEIGHTS = [(w_pairs_sb[:, :, :], w_pairs), (b_pairs_sb[:, :], b_pairs),
                   (w1z_sb[:, :, :], w1[0:D1, :].rearrange("(c p) o -> p c o", p=128)),
                   (w1c_sb[:, :], w1[D1:D1 + CTX, :]), (b1_sb[:, :], b1),
                   (w2_sb[:, :, :], w2.rearrange("(c p) o -> p c o", p=128)),
                   (b2_sb[:, :], b2), (w3_sb[:, :], w3)]

        block = ctx.enter_context(nc.Block())

        @block.sync
        def _(sp):
            with sp.Fori(0, STEPS) as step:
                for h in range(2):
                    first_row = sp.snap((step * 2 + h) * ROWS)
                    sp.wait_ge(product_ready, SEED + (step * 2 + h - 1) * UNITS)
                    sp.dma_start(rows_id[h][:, :], ids[bass.ds(first_row, ROWS), :])\
                      .then_inc(ids_loaded[h], 16)
                    sp.wait_ge(tail_mm, SEED + (step * 2 + h - 2) * TAIL_STAGES + 3)
                    sp.sem_inc(context_free, 1)
                    sp.dma_start(ctx_sb[h][:, :], ctx_t[:, bass.ds(first_row, ROWS)])\
                      .then_inc(ctx_loaded[h], 16)
            sp.wait_ge(tail_out, SEED + TILES * TAIL_STAGES)
            sp.dma_start(y, y_row[:, :]).then_inc(y_stored, 16)
            sp.wait_ge(y_stored, 16)

        @block.gpsimd
        def _(pool):
            pool.memset(ident[:, :], 0.0).then_inc(ident_ready, 1)
            pool.wait_ge(ident_ready, 1)
            pool.affine_select(out=ident[:, :], in_=ident[:, :], compare_op=ALU.not_equal, fill=1.0,
                               base=0, pattern=[[-1, 128]], channel_multiplier=1).then_inc(ident_ready, 1)
            with pool.Fori(0, STEPS) as step:
                for h in range(2):
                    pool.wait_ge(product_ready, SEED + (step * 2 + h - 1) * UNITS)
                    pool.wait_ge(ids_loaded[h], (step + 1) * 16)
                    pool.sem_inc(gathers_begun, 1)
                    for f in range(FIELDS):
                        pool.indirect_dma_start(
                            emb[h][:, f * DIM:(f + 1) * DIM], None, tables[f],
                            bass.IndirectOffsetOnAxis(rows_id[h][:, f:f + 1], 0),
                        ).then_inc(gathered[h][f // 2], 16)

        @block.tensor
        def _(pe):
            pe.wait_ge(ident_ready, 2)
            pe.wait_ge(zeroed, 4)

            def transpose_fields(step, h, m):
                pe.wait_ge(gathered[h][m], (step + 1) * 32)
                pe.wait_ge(emb_t_ready, SEED + (step * 2 + h) * (FIELDS // 2) + m)
                pe.transpose(emb_ps[:, 0:ROWS], emb[h][:, 2 * m * DIM:(2 * m + 2) * DIM],
                             ident[:, :]).then_inc(emb_in_psum, 1)

            def tail(step, h, stage):
                pe.wait_ge(tail_out, SEED + (step * 2 + h) * TAIL_STAGES + stage)
                if stage == 0:
                    pe.wait_ge(dve_summed, SEED + (step * 2 + h + 1) * DVE_SUMS)
                    pe.wait_ge(act_summed, SEED + (step * 2 + h + 1) * UNITS)
                    for c in range(PAIR_SPLIT):
                        done = pe.transpose(tail_ps[0:PBLOCK, c * ROWS:(c + 1) * ROWS],
                                            pij[h][:, c * PBLOCK:(c + 1) * PBLOCK], ident[:, :])
                if stage == 1:
                    pe.wait_ge(weights_loaded, 16 * len(WEIGHTS))
                    for o in range(D1 // 128):
                        for c in range(PAIR_SPLIT):
                            done = pe.matmul(tail_ps[:, o * ROWS:(o + 1) * ROWS],
                                             w_pairs_sb[:, c, o * 128:(o + 1) * 128], pij_t[:, c, :],
                                             start=c == 0, stop=c == PAIR_SPLIT - 1)
                if stage == 2:
                    pe.wait_ge(ctx_loaded[h], (step + 1) * 16)
                    for o in range(H1 // 128):
                        for c in range(D1 // 128):
                            pe.matmul(tail_ps[:, o * ROWS:(o + 1) * ROWS],
                                      w1z_sb[:, c, o * 128:(o + 1) * 128], z_t[:, c, :],
                                      start=c == 0, stop=False)
                        done = pe.matmul(tail_ps[:, o * ROWS:(o + 1) * ROWS],
                                         w1c_sb[:, o * 128:(o + 1) * 128], ctx_sb[h][:, :],
                                         start=False, stop=True)
                if stage == 3:
                    for o in range(H2 // 128):
                        for c in range(H1 // 128):
                            done = pe.matmul(tail_ps[:, o * ROWS:(o + 1) * ROWS],
                                             w2_sb[:, c, o * 128:(o + 1) * 128], h1_t[:, c, :],
                                             start=c == 0, stop=c == H1 // 128 - 1)
                if stage == 4:
                    for c in range(H2 // 128):
                        done = pe.matmul(tail_ps[0:1, 0:ROWS], w3_sb[:, c:c + 1], h2_t[:, c, :],
                                         start=c == 0, stop=c == H2 // 128 - 1)
                done.then_inc(tail_mm, 1)

            with pe.Fori(0, STEPS) as step:
                for h in range(2):
                    transpose_fields(step, h, 0)
                    for u, (j, i0, n, _) in enumerate(UNITS_OF):
                        if starts_pair(u):
                            if j // 2 + 1 < FIELDS // 2:
                                transpose_fields(step, h, j // 2 + 1)
                            pe.wait_ge(emb_t_ready, SEED + (step * 2 + h) * (FIELDS // 2) + j // 2 + 1)
                        at = first_column(j) + i0 * DIM
                        for c in range(at // KCHUNK, (at + n * DIM - 1) // KCHUNK + 1):
                            pe.wait_ge(k_loaded[c], 16)
                        pe.wait_ge(product_ready, SEED + (step * 2 + h) * UNITS + u - 1)
                        for a in range(0, n, 8):
                            w = min(8, n - a)
                            done = pe.matmul(t_ps[u % 2][:, a:a + w, :], emb_t[j // 2 % 2][j % 2][:, :],
                                             k_sb[:, at + a * DIM:at + (a + w) * DIM], start=True, stop=True)
                        done.then_inc(t_ready, 1)
                        if h == 1 and u in TAIL_AFTER:
                            tail(step, 0, TAIL_AFTER.index(u))
                for stage in range(TAIL_STAGES):
                    tail(step, 1, stage)

        @block.vector
        def _(dve):
            for s in range(2):
                for p in range(2):
                    dve.memset(emb_t[s][p][(1 - p) * DIM:(2 - p) * DIM, :], 0.0).then_inc(zeroed, 1)

            def sum_products(step, h, u):
                j, i0, n, by_act = UNITS_OF[u]
                if u == 0:
                    return
                dve.wait_ge(product_ready, SEED + (step * 2 + h) * UNITS + u + 1)
                q = j * (j - 1) // 2 + i0
                dve.tensor_reduce(pij[h][:, q:q + n - by_act],
                                  product[(h * UNITS + u) % PRODUCT_BUFFERS][:, 0:n - by_act, :], AX.X, ALU.add)\
                   .then_inc(dve_summed, 1)

            with dve.Fori(0, STEPS) as step:
                for h in range(2):
                    dve.wait_ge(tail_mm, SEED + (step * 2 + h - 2) * TAIL_STAGES + 1)
                    for u, (j, i0, n, _) in enumerate(UNITS_OF):
                        dve.wait_ge(t_ready, SEED + (step * 2 + h) * UNITS + u + 1)
                        dve.wait_ge(act_summed, SEED + (step * 2 + h) * UNITS + u + 1 - PRODUCT_BUFFERS)
                        before = u - PRODUCT_BUFFERS + (u < PRODUCT_BUFFERS)
                        dve.wait_ge(dve_summed, SEED + (step * 2 + h) * DVE_SUMS + before)
                        dve.tensor_tensor(
                            product[(h * UNITS + u) % PRODUCT_BUFFERS][:, 0:n, :], t_ps[u % 2][:, 0:n, :],
                            emb[h][:, i0 * DIM:(i0 + n) * DIM].rearrange("p (i e) -> p i e", e=DIM),
                            ALU.mult).then_inc(product_ready, 1)
                        if u > 0:
                            sum_products(step, h, u - 1)
                    sum_products(step, h, UNITS - 1)

        @block.scalar
        def _(act):
            for s in (product_ready, act_summed, dve_summed, t_ready, emb_t_ready, tail_mm, tail_out):
                act.nop().then_inc(s, SEED)
            for c in range(KCHUNKS):
                act.dma_start(k_sb[:, c * KCHUNK:(c + 1) * KCHUNK],
                              k_cols[:, c * KCHUNK:(c + 1) * KCHUNK]).then_inc(k_loaded[c], 16)
            for to, of in WEIGHTS:
                act.dma_start(to, of).then_inc(weights_loaded, 16)

            def copy_fields(step, h, m):
                tile = step * 2 + h
                act.wait_ge(emb_in_psum, tile * (FIELDS // 2) + m + 1)
                if m >= 2:
                    act.wait_ge(t_ready, SEED + tile * UNITS + last_unit(m - 2) + 1)
                else:
                    act.wait_ge(t_ready, SEED + (tile - 1) * UNITS + last_unit(m - 2 + FIELDS // 2) + 1)
                act.copy(emb_t[m % 2][0][0:DIM, :], emb_ps[0:DIM, 0:ROWS])
                act.copy(emb_t[m % 2][1][DIM:2 * DIM, :], emb_ps[DIM:2 * DIM, 0:ROWS])\
                   .then_inc(emb_t_ready, 1)

            def sum_products(step, h, u):
                j, i0, n, by_act = UNITS_OF[u]
                act.wait_ge(product_ready, SEED + (step * 2 + h) * UNITS + u + 1)
                q = j * (j - 1) // 2 + i0
                for i in range(n - by_act, n):
                    terms = product[(h * UNITS + u) % PRODUCT_BUFFERS][:, i, :]
                    done = act.activation(terms, terms, ACT.Copy,
                                          accum_out=pij[h][:, q + i:q + i + 1])
                done.then_inc(act_summed, 1)

            def tail(step, h, stage):
                act.wait_ge(tail_mm, SEED + (step * 2 + h) * TAIL_STAGES + stage + 1)
                if stage == 0:
                    done = act.copy(pij_t[:, :, :].rearrange("q c b -> q (c b)"), tail_ps[0:PBLOCK, :])
                if stage == 1:
                    act.wait_ge(weights_loaded, 16 * len(WEIGHTS))
                    for o in range(D1 // 128):
                        done = act.activation(z_t[:, o, :], tail_ps[:, o * ROWS:(o + 1) * ROWS],
                                              ACT.Identity, bias=b_pairs_sb[:, o:o + 1])
                if stage == 2:
                    for o in range(H1 // 128):
                        done = act.activation(h1_t[:, o, :], tail_ps[:, o * ROWS:(o + 1) * ROWS],
                                              ACT.Relu, bias=b1_sb[:, o:o + 1])
                if stage == 3:
                    for o in range(H2 // 128):
                        done = act.activation(h2_t[:, o, :], tail_ps[:, o * ROWS:(o + 1) * ROWS],
                                              ACT.Relu, bias=b2_sb[:, o:o + 1])
                if stage == 4:
                    done = act.copy(y_row[:, bass.ds((step * 2 + h) * ROWS, ROWS)], tail_ps[0:1, 0:ROWS])
                done.then_inc(tail_out, 1)

            with act.Fori(0, STEPS) as step:
                for h in range(2):
                    copy_fields(step, h, 0)
                    for u, (j, i0, n, _) in enumerate(UNITS_OF):
                        if starts_pair(u) and j // 2 + 1 < FIELDS // 2:
                            copy_fields(step, h, j // 2 + 1)
                        sum_products(step, h, u)
                        if h == 1 and u in TAIL_AFTER:
                            tail(step, 0, TAIL_AFTER.index(u))
                for stage in range(TAIL_STAGES):
                    tail(step, 1, stage)


def kernel(dense_ctx, ids, W_top1, b_top1, W_top2, b_top2, W_top3, L0_rec_kernel, L0_rec_W, L0_rec_b,
           **tbl):
    import numpy as np
    import concourse.bacc as bacc
    from concourse.bass_utils import run_bass_kernel_spmd

    def columns(v):
        return np.ascontiguousarray(np.asarray(v).reshape(-1, 128).T)

    i, j = np.triu_indices(FIELDS, k=1)
    number = {(int(a), int(b)): p for p, (a, b) in enumerate(zip(i, j))}
    order = [number[a, b] for b in range(FIELDS) for a in range(b)]
    kern = np.asarray(L0_rec_kernel)[:, order, :].reshape(DIM, PAIRS * DIM)
    k_cols = np.zeros((128, KCOLS), kern.dtype)
    for f in range(1, FIELDS):
        at, q, half = first_column(f), f * (f - 1) // 2 * DIM, f % 2 * DIM
        k_cols[half:half + DIM, at:at + f * DIM] = kern[:, q:q + f * DIM]
    w_pairs = np.asarray(L0_rec_W)[:, order].T.reshape(PAIR_SPLIT, PBLOCK, D1).transpose(1, 0, 2)

    arrays = {f"tbl_{f}": np.asarray(tbl[f"tbl_{f}"]) for f in range(FIELDS)}
    arrays |= {
        "ids": np.asarray(ids), "k_cols": k_cols, "w_pairs": np.ascontiguousarray(w_pairs),
        "b_pairs": columns(L0_rec_b), "ctx_t": np.ascontiguousarray(np.asarray(dense_ctx).T),
        "w1": np.asarray(W_top1), "b1": columns(b_top1), "w2": np.asarray(W_top2),
        "b2": columns(b_top2), "w3": columns(W_top3),
    }
    nc = bacc.Bacc("TRN2", target_bir_lowering=False, num_devices=1)
    given = {name: nc.dram_tensor(name, a.shape, mybir.dt.from_np(a.dtype), kind="ExternalInput").ap()
             for name, a in arrays.items()}
    y = nc.dram_tensor("y", (1, BATCH), mybir.dt.float32, kind="ExternalOutput").ap()
    tables = [given.pop(f"tbl_{f}") for f in range(FIELDS)]
    build(nc, tables, *given.values(), y)
    got = run_bass_kernel_spmd(nc, [arrays], core_ids=[0])
    return got.results[0]["y"].reshape(BATCH, 1)
```

```python
from contextlib import ExitStack

import concourse.bass as bass
from concourse import mybir

FIELDS, DIM = 32, 64
PAIRS = FIELDS * (FIELDS - 1) // 2
PAIR_SPLIT = 4
PBLOCK = PAIRS // PAIR_SPLIT
BATCH, ROWS = 512, 128
TILES = BATCH // ROWS
STEPS = TILES // 2
D1, CTX, H1, H2 = 256, 16, 512, 256
GROUP = 4
GROUPS = FIELDS // GROUP
MIXED_FROM = 4
SPLIT_FIELDS = [j for j in range(FIELDS) if j // GROUP >= MIXED_FROM and j % GROUP >= GROUP // 2]
WHOLE_FIELDS = [j for j in range(1, FIELDS) if j not in SPLIT_FIELDS]
MIXED_GROUPS = GROUPS - MIXED_FROM
ACT_SHARE = 0.48
POOL_UNITS = (21, 24, 27, 30, 33, 36, 39, 42)
EARLY_GATHERS = 16
POOL_LEVELS = (32, 16, 8)
POOL_LAG = 5
KCHUNK = 16 * DIM
RAW_BUFFERS = 3


def first_column(j):
    return sum(k for k in WHOLE_FIELDS if k < j and k % 2 == j % 2) * DIM


def first_split_column(j):
    return sum(k for k in SPLIT_FIELDS if k < j) * DIM


KCOLS = max(first_column(j) + j * DIM for j in WHOLE_FIELDS)
KCHUNKS = -(-KCOLS // KCHUNK)
SPLIT_COLS = first_split_column(FIELDS)


def cut_units():
    order = []
    for group in range(GROUPS):
        kinds = [], []
        for j in range(max(1, group * GROUP), (group + 1) * GROUP):
            parts = 1 if j <= 16 else 2 if j < FIELDS - 2 else 3
            edges = [j * c // parts for c in range(parts + 1)]
            kinds[j in SPLIT_FIELDS].extend((j, a, b - a) for a, b in zip(edges, edges[1:]))
        for c in range(max(map(len, kinds))):
            order += [kind[c] for kind in kinds if c < len(kind)]
    return order


UNITS_OF = cut_units()
UNITS = len(UNITS_OF)
SEED = 2 * UNITS
T_BUFFERS = 3
PRODUCT_BUFFERS = 8
assert UNITS % T_BUFFERS == 0 and UNITS % PRODUCT_BUFFERS == 0
TAIL_STAGES = 5
TAIL_PARTS = {14: (0, 0, 4), 19: (1, 0, 1), 20: (1, 1, 2), 24: (2, 0, 1), 25: (2, 1, 2), 27: (2, 2, 3),
              28: (2, 3, 4), 34: (3, 0, 1), 35: (3, 1, 2), 40: (4, 0, 1)}
TAIL_BLOCKS = (PAIR_SPLIT, D1 // 128, H1 // 128, H2 // 128, 1)


def act_pairs(u):
    if u in POOL_UNITS:
        return 0
    pairs = [0 if v in POOL_UNITS else UNITS_OF[v][2] for v in range(u + 1)]
    share = round(sum(pairs) * ACT_SHARE) - round(sum(pairs[:u]) * ACT_SHARE)
    return min(max(1, share), max(1, UNITS_OF[u][2] - 1))


def sums_behind(u):
    own = [u - 1] if u > 1 and u - 1 not in POOL_UNITS else []
    pooled = [u - POOL_LAG] if u - POOL_LAG in POOL_UNITS else []
    return own + pooled + ([u] if u == UNITS - 1 else [])


DVE_ORDER = [v for u in range(UNITS) for v in sums_behind(u)]
ACT_ORDER = [u for u in range(UNITS) if u not in POOL_UNITS]
assert sorted(DVE_ORDER) == list(range(1, UNITS)) and POOL_LAG < PRODUCT_BUFFERS


def summed(order, u):
    if u < 0:
        return summed(order, u + UNITS) - len(order)
    while u >= 0 and u not in order:
        u -= 1
    return order.index(u) + 1 if u >= 0 else 0


ROWS_AT = {2: 3, 6: 4, 14: 5, 21: 6, 29: 7, 37: 0, 41: 1, 45: 2}
FIRST_ROWS_AT = {0: 1, 3: 2, 7: 3, 9: 4, 14: 5, 21: 6, 29: 7, 37: 0, 41: 1, 45: 2}
NEXT_TILE_FROM = 37
ROWS_LAG = 2
ROW_SLOTS = 4


def begins_group(u):
    group = UNITS_OF[u][0] // GROUP
    return group if u == 0 or UNITS_OF[u - 1][0] // GROUP != group else None


def rows_at(eng, step, h, u, do, lag=0):
    group, first = ROWS_AT.get(u - lag), FIRST_ROWS_AT.get(u - lag)
    if h == 0 and group != first:
        if first is not None:
            with eng.If(step < 1):
                do(step, h, first)
        if group is not None:
            with eng.If(step > 0):
                do(step, h, group)
    elif group is not None and u - lag < NEXT_TILE_FROM:
        do(step, h, group)
    elif group is not None and h == 0:
        do(step, 1, group)
    elif group is not None:
        with eng.If(step < STEPS - 1):
            do(step + 1, 0, group)


def units_through(group):
    if group < 0:
        return units_through(group + GROUPS) - UNITS
    return sum(j // GROUP <= group for j, *_ in UNITS_OF)


SPLIT_AHEAD = 3
SPLIT_LAG = 1
SPLIT_AT = {3 * c: j for c, j in enumerate(SPLIT_FIELDS[SPLIT_AHEAD:])}


def build(nc, tables, ids, k_cols, k_twice, w_pairs, b_pairs, ctx_t, w1, b1, w2, b2, w3, y):
    f32, f32r, i32 = mybir.dt.float32, mybir.dt.float32r, mybir.dt.int32
    ALU, ACT, AX = mybir.AluOpType, mybir.ActivationFunctionType, mybir.AxisListType

    ctx = ExitStack()
    with ctx:
        def sb(name, shape, dt=f32):
            return ctx.enter_context(nc.sbuf_tensor(name, shape, dt))

        def sem(name):
            return ctx.enter_context(nc.semaphore(name))

        k_sb = sb("k_sb", [128, KCOLS])
        ids_sb = sb("ids_sb", [ROWS, TILES + 1, FIELDS], i32)
        rows_id = [sb(f"rows_id{h}", [ROWS, FIELDS], i32) for h in range(2)]
        emb = [sb(f"emb{h}", [ROWS, FIELDS * DIM]) for h in range(2)]
        emb_t = [[sb(f"emb_t{s}{p}", [128, GROUP // 2 * ROWS]) for p in range(2)] for s in range(ROW_SLOTS)]
        emb_parts = [[sb(f"emb_parts{s}{p}", [128, 2, ROWS], f32r) for p in range(2)] for s in range(2)]
        k_raw = [sb(f"k_raw{r}", [128, (FIELDS - 1) * DIM]) for r in range(RAW_BUFFERS)]
        k_split = sb("k_split", [128, SPLIT_COLS], f32r)
        product = [sb(f"product{g}", [ROWS, 16, DIM]) for g in range(PRODUCT_BUFFERS)]
        pij = [sb(f"pij{h}", [ROWS, PAIRS]) for h in range(2)]
        pij_t = sb("pij_t", [PBLOCK, PAIR_SPLIT, ROWS])
        z_t = sb("z_t", [128, D1 // 128, ROWS])
        h1_t = sb("h1_t", [128, H1 // 128, ROWS])
        h2_t = sb("h2_t", [128, H2 // 128, ROWS])
        y_row = sb("y_row", [1, ROWS + BATCH])
        ident = sb("ident", [128, 128])
        w_pairs_sb = sb("w_pairs_sb", [PBLOCK, PAIR_SPLIT, D1])
        b_pairs_sb = sb("b_pairs_sb", [128, D1 // 128])
        ctx_sb = sb("ctx_sb", [CTX, ROWS + BATCH])
        w1z_sb = sb("w1z_sb", [128, D1 // 128, H1])
        w1c_sb = sb("w1c_sb", [CTX, H1])
        b1_sb = sb("b1_sb", [128, H1 // 128])
        w2_sb = sb("w2_sb", [128, H1 // 128, H2])
        b2_sb = sb("b2_sb", [128, H2 // 128])
        w3_sb = sb("w3_sb", [128, H2 // 128])

        t_ps = [ctx.enter_context(nc.psum_tensor(f"t_ps{p}", [ROWS, 16, DIM], f32))
                for p in range(T_BUFFERS)]
        emb_ps = ctx.enter_context(nc.psum_tensor("emb_ps", [128, 512], f32))
        tail_ps = ctx.enter_context(nc.psum_tensor("tail_ps", [128, 512], f32))

        ids_loaded = sem("ids_loaded")
        ids_copied = sem("ids_copied")
        gathered = [[sem(f"gathered{h}_{g}") for g in range(GROUPS)] for h in range(2)]
        k_loaded = [sem(f"k_loaded{c}") for c in range(KCHUNKS)]
        raw_loaded = [sem(f"raw_loaded{r}") for r in range(RAW_BUFFERS)]
        k_hi_ready = sem("k_hi_ready")
        k_split_ready = sem("k_split_ready")
        pool_added = sem("pool_added")
        weights_loaded = sem("weights_loaded")
        zeroed = sem("zeroed")
        ident_ready = sem("ident_ready")
        emb_in_psum = sem("emb_in_psum")
        emb_copied = sem("emb_copied")
        emb_split = sem("emb_split")
        rows_doubled = [sem(f"rows_doubled{s}") for s in range(2)]
        t_ready = sem("t_ready")
        product_ready = sem("product_ready")
        act_summed = sem("act_summed")
        dve_summed = sem("dve_summed")
        tail_mm = sem("tail_mm")
        tail_out = sem("tail_out")
        y_stored = sem("y_stored")
        gathers_begun = sem("gathers_begun")

        WEIGHTS = [(w_pairs_sb[:, :, :], w_pairs), (b_pairs_sb[:, :], b_pairs),
                   (w1z_sb[:, :, :], w1[0:D1, :].rearrange("(c p) o -> p c o", p=128)),
                   (ctx_sb[:, :], ctx_t), (w1c_sb[:, :], w1[D1:D1 + CTX, :]), (b1_sb[:, :], b1),
                   (w2_sb[:, :, :], w2.rearrange("(c p) o -> p c o", p=128)),
                   (b2_sb[:, :], b2), (w3_sb[:, :], w3)]

        block = ctx.enter_context(nc.Block())

        @block.sync
        def _(sp):
            sp.dma_start(ids_sb[:, 0:TILES, :], ids.rearrange("(t b) f -> b t f", b=ROWS)).then_inc(ids_loaded, 16)
            for c in range(KCHUNKS):
                if c >= 1:
                    sp.wait_ge(gathered[0][min(c - 1, GROUPS - 2)], 16 * GROUP)
                cols = slice(c * KCHUNK, min((c + 1) * KCHUNK, KCOLS))
                sp.dma_start(k_sb[:, cols], k_cols[:, cols]).then_inc(k_loaded[c], 16)
            with sp.Fori(0, STEPS) as step:
                for h in range(2):
                    for c in range(MIXED_GROUPS):
                        slot = (MIXED_FROM + c) % 2
                        sp.wait_ge(emb_split, SEED + (step * 2 + h) * MIXED_GROUPS + c + 1)
                        for p in range(2):
                            own, other = slice(p * DIM, (p + 1) * DIM), slice((1 - p) * DIM, (2 - p) * DIM)
                            parts = emb_parts[slot][p]
                            sp.dma_start(parts[other, :, :].bitcast(f32), parts[own, :, :].bitcast(f32))\
                              .then_inc(rows_doubled[slot], 16)
                        if h == 0 and c == 0:
                            with sp.If(step < 1):
                                for to, of in WEIGHTS:
                                    sp.dma_start(to, of).then_inc(weights_loaded, 16)
            sp.wait_ge(tail_out, SEED + (TILES + 1) * TAIL_STAGES)
            sp.dma_start(y, y_row[:, ROWS:ROWS + BATCH]).then_inc(y_stored, 16)
            sp.wait_ge(y_stored, 16)

        @block.gpsimd
        def _(pool):
            pool.memset(ident[:, :], 0.0).then_inc(ident_ready, 1)
            pool.wait_ge(ident_ready, 1)
            pool.affine_select(out=ident[:, :], in_=ident[:, :], compare_op=ALU.not_equal, fill=1.0,
                               base=0, pattern=[[-1, 128]], channel_multiplier=1).then_inc(ident_ready, 1)
            pool.wait_ge(ids_loaded, 16)

            def begin_gathers(step, h):
                pool.wait_ge(product_ready, SEED + (step * 2 + h - 1) * UNITS)
                pool.tensor_copy(rows_id[h][:, :], ids_sb[:, bass.ds(step * 2 + h, 1), :]
                                 if not isinstance(step, int) else ids_sb[:, step * 2 + h, :])\
                    .then_inc(ids_copied, 1)
                pool.wait_ge(ids_copied, step * 2 + h + 1)
                pool.sem_inc(gathers_begun, 1)

            def gather(h, fields):
                for f in fields:
                    pool.indirect_dma_start(
                        emb[h][:, f * DIM:(f + 1) * DIM], None, tables[f],
                        bass.IndirectOffsetOnAxis(rows_id[h][:, f:f + 1], 0),
                    ).then_inc(gathered[h][f // GROUP], 16)

            def add_products(step, h, u):
                tile, n = step * 2 + h, UNITS_OF[u][2]
                pool.wait_ge(product_ready, SEED + tile * UNITS + u + 1)
                for c, left in enumerate(POOL_LEVELS):
                    begun = (tile * len(POOL_UNITS) + POOL_UNITS.index(u)) * len(POOL_LEVELS) + c
                    terms = product[u % PRODUCT_BUFFERS]
                    if c > 0:
                        pool.wait_ge(pool_added, begun)
                    pool.tensor_tensor(terms[:, 0:n, 0:left], terms[:, 0:n, 0:left],
                                       terms[:, 0:n, left:2 * left], ALU.add).then_inc(pool_added, 1)

            def gather_next(step, h, fields):
                if h == 0:
                    gather(1, fields)
                else:
                    with pool.If(step < STEPS - 1):
                        gather(0, fields)

            begin_gathers(0, 0)
            gather(0, range(FIELDS))
            with pool.Fori(0, STEPS) as step:
                for h in range(2):
                    if h == 0:
                        begin_gathers(step, 1)
                    else:
                        with pool.If(step < STEPS - 1):
                            begin_gathers(step + 1, 0)
                    gather_next(step, h, range(EARLY_GATHERS))
                    each = (FIELDS - EARLY_GATHERS) // len(POOL_UNITS)
                    for c, u in enumerate(POOL_UNITS):
                        add_products(step, h, u)
                        gather_next(step, h, range(EARLY_GATHERS + c * each, EARLY_GATHERS + (c + 1) * each))

        @block.tensor
        def _(pe):
            pe.wait_ge(ident_ready, 2)
            pe.wait_ge(zeroed, 2 * ROW_SLOTS + 1)

            def transpose_rows(step, h, group):
                pe.wait_ge(emb_copied, SEED + (step * 2 + h) * GROUPS + group)
                splits = max(0, group - MIXED_FROM)
                pe.wait_ge(emb_split, SEED + (step * 2 + h) * MIXED_GROUPS + splits)
                pe.wait_ge(gathered[h][group], (step + 1) * 16 * GROUP)
                for m in range(GROUP // 2):
                    at = (group * GROUP + 2 * m) * DIM
                    done = pe.transpose(emb_ps[:, m * ROWS:(m + 1) * ROWS], emb[h][:, at:at + 2 * DIM], ident[:, :])
                done.then_inc(emb_in_psum, 1)

            def tail(tile, before, stage, first, end):
                if first == 0:
                    pe.wait_ge(tail_out, SEED + tile * TAIL_STAGES + stage)
                if stage == 0:
                    pe.wait_ge(dve_summed, SEED + tile * len(DVE_ORDER))
                    pe.wait_ge(act_summed, SEED + tile * len(ACT_ORDER))
                    for c in range(first, end):
                        done = pe.transpose(tail_ps[0:PBLOCK, c * ROWS:(c + 1) * ROWS],
                                            pij[before][:, c * PBLOCK:(c + 1) * PBLOCK], ident[:, :])
                if stage == 1:
                    pe.wait_ge(weights_loaded, 16 * len(WEIGHTS))
                    for o in range(first, end):
                        for c in range(PAIR_SPLIT):
                            done = pe.matmul(tail_ps[:, o * ROWS:(o + 1) * ROWS],
                                             w_pairs_sb[:, c, o * 128:(o + 1) * 128], pij_t[:, c, :],
                                             start=c == 0, stop=c == PAIR_SPLIT - 1)
                if stage == 2:
                    for o in range(first, end):
                        for c in range(D1 // 128):
                            pe.matmul(tail_ps[:, o * ROWS:(o + 1) * ROWS],
                                      w1z_sb[:, c, o * 128:(o + 1) * 128], z_t[:, c, :],
                                      start=c == 0, stop=False)
                        done = pe.matmul(tail_ps[:, o * ROWS:(o + 1) * ROWS],
                                         w1c_sb[:, o * 128:(o + 1) * 128],
                                         ctx_sb[:, bass.ds(tile * ROWS, ROWS)],
                                         start=False, stop=True)
                if stage == 3:
                    for o in range(first, end):
                        for c in range(H1 // 128):
                            done = pe.matmul(tail_ps[:, o * ROWS:(o + 1) * ROWS],
                                             w2_sb[:, c, o * 128:(o + 1) * 128], h1_t[:, c, :],
                                             start=c == 0, stop=c == H1 // 128 - 1)
                if stage == 4:
                    for c in range(H2 // 128):
                        done = pe.matmul(tail_ps[0:1, 0:ROWS], w3_sb[:, c:c + 1], h2_t[:, c, :],
                                         start=c == 0, stop=c == H2 // 128 - 1)
                if end == TAIL_BLOCKS[stage]:
                    done.then_inc(tail_mm, 1)

            transpose_rows(0, 0, 0)
            with pe.Fori(0, STEPS) as step:
                for h in range(2):
                    for u, (j, i0, n) in enumerate(UNITS_OF):
                        rows_at(pe, step, h, u, transpose_rows)
                        group = begins_group(u)
                        if group is not None:
                            pe.wait_ge(emb_copied, SEED + (step * 2 + h) * GROUPS + group + 1)
                            if group >= MIXED_FROM:
                                before = (group - MIXED_FROM) // 2
                                pe.wait_ge(rows_doubled[group % 2],
                                           ((step * 2 + h) * MIXED_GROUPS // 2 + before + 1) * 32)
                        pe.wait_ge(product_ready, SEED + (step * 2 + h) * UNITS + u + 1 - T_BUFFERS)
                        banks = [(a, min(8, n - a)) for a in range(0, n, 8)]
                        place = j % GROUP // 2
                        if j in WHOLE_FIELDS:
                            at = first_column(j) + i0 * DIM
                            for c in range(at // KCHUNK, (at + n * DIM - 1) // KCHUNK + 1):
                                pe.wait_ge(k_loaded[c], 16)
                            for a, w in banks:
                                done = pe.matmul(t_ps[u % T_BUFFERS][:, a:a + w, :],
                                                 emb_t[j // GROUP % ROW_SLOTS][j % 2][:, place * ROWS:(place + 1) * ROWS],
                                                 k_sb[:, at + a * DIM:at + (a + w) * DIM],
                                                 start=True, stop=True)
                        else:
                            at = first_split_column(j) + i0 * DIM
                            pe.wait_ge(k_split_ready, SPLIT_FIELDS.index(j) + 1)
                            for part in range(2):
                                for a, w in banks:
                                    done = pe.matmul(t_ps[u % T_BUFFERS][:, a:a + w, :],
                                                     emb_parts[j // GROUP % 2][j % 2][:, part, :],
                                                     k_split[:, at + a * DIM:at + (a + w) * DIM],
                                                     start=part == 0, stop=part == 1)
                        done.then_inc(t_ready, 1)
                        if u in TAIL_PARTS:
                            tail(step * 2 + h, 1 - h, *TAIL_PARTS[u])
            for stage in range(TAIL_STAGES):
                tail(TILES, 1, stage, 0, TAIL_BLOCKS[stage])

        @block.vector
        def _(dve):
            for s in range(ROW_SLOTS):
                for p in range(2):
                    dve.memset(emb_t[s][p][(1 - p) * DIM:(2 - p) * DIM, :], 0.0).then_inc(zeroed, 1)
            dve.memset(pij[1][:, :], 0.0).then_inc(zeroed, 1)

            def sum_products(step, h, u):
                j, i0, n = UNITS_OF[u]
                tile, n = step * 2 + h, n - act_pairs(u)
                terms = product[u % PRODUCT_BUFFERS][:, 0:n, :]
                if u in POOL_UNITS:
                    done = (tile * len(POOL_UNITS) + POOL_UNITS.index(u) + 1) * len(POOL_LEVELS)
                    dve.wait_ge(pool_added, done)
                    terms = product[u % PRODUCT_BUFFERS][:, 0:n, 0:POOL_LEVELS[-1]]
                dve.wait_ge(product_ready, SEED + tile * UNITS + u + 1)
                q = j * (j - 1) // 2 + i0
                dve.tensor_reduce(pij[h][:, q:q + n], terms, AX.X, ALU.add).then_inc(dve_summed, 1)

            def split_kernel(j):
                c, at = SPLIT_FIELDS.index(j), first_split_column(j)
                dve.wait_ge(k_hi_ready, c + 1)
                low = k_split[DIM:2 * DIM, at:at + j * DIM]
                dve.tensor_tensor(low, k_raw[c % RAW_BUFFERS][DIM:2 * DIM, 0:j * DIM],
                                  low.bitcast(f32), ALU.subtract).then_inc(k_split_ready, 1)

            def split_rows(step, h, group):
                if group < MIXED_FROM:
                    return
                """The lo parts of a group's split fields' transposed rows: what the hi parts leave."""
                dve.wait_ge(emb_copied, SEED + (step * 2 + h) * GROUPS + group + 1)
                for p in range(2):
                    parts, own = emb_parts[group % 2][p], slice(p * DIM, (p + 1) * DIM)
                    done = dve.tensor_tensor(parts[own, 1, :], emb_ps[own, ROWS:2 * ROWS],
                                             parts[own, 0, :].bitcast(f32), ALU.subtract)
                done.then_inc(emb_split, 1)

            for j in SPLIT_FIELDS[:SPLIT_AHEAD]:
                split_kernel(j)
            with dve.Fori(0, STEPS) as step:
                for h in range(2):
                    dve.wait_ge(tail_mm, SEED + (step * 2 + h - 1) * TAIL_STAGES + 1)
                    for u, (j, i0, n) in enumerate(UNITS_OF):
                        tile, before = step * 2 + h, u - PRODUCT_BUFFERS
                        dve.wait_ge(t_ready, SEED + tile * UNITS + u + 1)
                        dve.wait_ge(act_summed, SEED + tile * len(ACT_ORDER) + summed(ACT_ORDER, before))
                        dve.wait_ge(dve_summed, SEED + tile * len(DVE_ORDER) + summed(DVE_ORDER, before))
                        dve.tensor_tensor(
                            product[u % PRODUCT_BUFFERS][:, 0:n, :], t_ps[u % T_BUFFERS][:, 0:n, :],
                            emb[h][:, i0 * DIM:(i0 + n) * DIM].rearrange("p (i e) -> p i e", e=DIM),
                            ALU.mult).then_inc(product_ready, 1)
                        if ROWS_AT.get(u - ROWS_LAG, 0) >= MIXED_FROM or FIRST_ROWS_AT.get(u - ROWS_LAG, 0) >= MIXED_FROM:
                            rows_at(dve, step, h, u, split_rows, ROWS_LAG)
                        for v in sums_behind(u):
                            sum_products(step, h, v)
                        if h == 0 and u - SPLIT_LAG in SPLIT_AT:
                            with dve.If(step < 1):
                                split_kernel(SPLIT_AT[u - SPLIT_LAG])

        @block.scalar
        def _(act):
            def load_raw(c):
                at, cols = first_split_column(SPLIT_FIELDS[c]), SPLIT_FIELDS[c] * DIM
                act.dma_start(k_raw[c % RAW_BUFFERS][:, 0:cols], k_twice[:, at:at + cols])\
                   .then_inc(raw_loaded[c % RAW_BUFFERS], 16)

            for c in range(RAW_BUFFERS):
                load_raw(c)
            for s in (product_ready, act_summed, dve_summed, t_ready, emb_copied, emb_split, tail_mm, tail_out):
                act.nop().then_inc(s, SEED)

            def copy_rows(step, h, group):
                tile = step * 2 + h
                act.wait_ge(emb_in_psum, tile * GROUPS + group + 1)
                held = group - ROW_SLOTS
                if group >= MIXED_FROM:
                    held = max(held, group - 2 if group - 2 >= MIXED_FROM else group + 2 - GROUPS)
                act.wait_ge(t_ready, SEED + tile * UNITS + units_through(held))
                for p in range(2):
                    own = slice(p * DIM, (p + 1) * DIM)
                    wholes = ROWS if group >= MIXED_FROM else 2 * ROWS
                    done = act.copy(emb_t[group % ROW_SLOTS][p][own, 0:wholes], emb_ps[own, 0:wholes])
                    if group >= MIXED_FROM:
                        done = act.copy(emb_parts[group % 2][p][own, 0, :], emb_ps[own, ROWS:2 * ROWS])
                done.then_inc(emb_copied, 1)

            def split_kernel(j):
                c, at = SPLIT_FIELDS.index(j), first_split_column(j)
                act.wait_ge(raw_loaded[c % RAW_BUFFERS], 16 * (c // RAW_BUFFERS + 1))
                act.copy(k_split[:, at:at + j * DIM], k_raw[c % RAW_BUFFERS][:, 0:j * DIM]).then_inc(k_hi_ready, 1)
                if 1 <= c <= len(SPLIT_FIELDS) - RAW_BUFFERS:
                    act.wait_ge(k_split_ready, c)
                    load_raw(c + RAW_BUFFERS - 1)

            def sum_products(step, h, u):
                j, i0, n = UNITS_OF[u]
                act.wait_ge(product_ready, SEED + (step * 2 + h) * UNITS + u + 1)
                q = j * (j - 1) // 2 + i0
                for i in range(n - act_pairs(u), n):
                    terms = product[u % PRODUCT_BUFFERS][:, i, :]
                    done = act.activation(terms, terms, ACT.Copy, accum_out=pij[h][:, q + i:q + i + 1])
                done.then_inc(act_summed, 1)

            def tail(tile, stage):
                act.wait_ge(tail_mm, SEED + tile * TAIL_STAGES + stage + 1)
                if stage == 0:
                    done = act.copy(pij_t[:, :, :].rearrange("q c b -> q (c b)"), tail_ps[0:PBLOCK, :])
                if stage == 1:
                    act.wait_ge(weights_loaded, 16 * len(WEIGHTS))
                    for o in range(D1 // 128):
                        done = act.activation(z_t[:, o, :], tail_ps[:, o * ROWS:(o + 1) * ROWS],
                                              ACT.Identity, bias=b_pairs_sb[:, o:o + 1])
                if stage == 2:
                    for o in range(H1 // 128):
                        done = act.activation(h1_t[:, o, :], tail_ps[:, o * ROWS:(o + 1) * ROWS],
                                              ACT.Relu, bias=b1_sb[:, o:o + 1])
                if stage == 3:
                    for o in range(H2 // 128):
                        done = act.activation(h2_t[:, o, :], tail_ps[:, o * ROWS:(o + 1) * ROWS],
                                              ACT.Relu, bias=b2_sb[:, o:o + 1])
                if stage == 4:
                    done = act.copy(y_row[:, bass.ds(tile * ROWS, ROWS)] if not isinstance(tile, int) else
                                    y_row[:, tile * ROWS:(tile + 1) * ROWS], tail_ps[0:1, 0:ROWS])
                done.then_inc(tail_out, 1)

            for j in SPLIT_FIELDS[:SPLIT_AHEAD]:
                split_kernel(j)
            copy_rows(0, 0, 0)
            with act.Fori(0, STEPS) as step:
                for h in range(2):
                    for u, (j, i0, n) in enumerate(UNITS_OF):
                        if h == 0 and u in SPLIT_AT:
                            with act.If(step < 1):
                                split_kernel(SPLIT_AT[u])
                        rows_at(act, step, h, u, copy_rows)
                        if u not in POOL_UNITS:
                            sum_products(step, h, u)
                        if u in TAIL_PARTS:
                            stage, _, end = TAIL_PARTS[u]
                            if end == TAIL_BLOCKS[stage]:
                                tail(step * 2 + h, stage)
            for stage in range(TAIL_STAGES):
                tail(TILES, stage)


def kernel(dense_ctx, ids, W_top1, b_top1, W_top2, b_top2, W_top3, L0_rec_kernel, L0_rec_W, L0_rec_b,
           **tbl):
    import numpy as np
    import concourse.bacc as bacc
    from concourse.bass_utils import run_bass_kernel_spmd

    def columns(v):
        return np.ascontiguousarray(np.asarray(v).reshape(-1, 128).T)

    i, j = np.triu_indices(FIELDS, k=1)
    number = {(int(a), int(b)): p for p, (a, b) in enumerate(zip(i, j))}
    order = [number[a, b] for b in range(FIELDS) for a in range(b)]
    kern = np.asarray(L0_rec_kernel)[:, order, :].reshape(DIM, PAIRS * DIM)
    k_cols = np.zeros((128, KCOLS), kern.dtype)
    for f in WHOLE_FIELDS:
        at, q, half = first_column(f), f * (f - 1) // 2 * DIM, f % 2 * DIM
        k_cols[half:half + DIM, at:at + f * DIM] = kern[:, q:q + f * DIM]
    split = [kern[:, f * (f - 1) // 2 * DIM:f * (f + 1) // 2 * DIM] for f in SPLIT_FIELDS]
    k_twice = np.concatenate([np.concatenate(split, axis=1)] * 2)
    w_pairs = np.asarray(L0_rec_W)[:, order].T.reshape(PAIR_SPLIT, PBLOCK, D1).transpose(1, 0, 2)

    ctx_t = np.zeros((CTX, ROWS + BATCH), np.asarray(dense_ctx).dtype)
    ctx_t[:, ROWS:] = np.asarray(dense_ctx).T

    arrays = {f"tbl_{f}": np.asarray(tbl[f"tbl_{f}"]) for f in range(FIELDS)}
    arrays |= {
        "ids": np.asarray(ids), "k_cols": k_cols, "k_twice": k_twice, "w_pairs": np.ascontiguousarray(w_pairs),
        "b_pairs": columns(L0_rec_b), "ctx_t": ctx_t,
        "w1": np.asarray(W_top1), "b1": columns(b_top1), "w2": np.asarray(W_top2),
        "b2": columns(b_top2), "w3": columns(W_top3),
    }
    nc = bacc.Bacc("TRN2", target_bir_lowering=False, num_devices=1)
    given = {name: nc.dram_tensor(name, a.shape, mybir.dt.from_np(a.dtype), kind="ExternalInput").ap()
             for name, a in arrays.items()}
    y = nc.dram_tensor("y", (1, BATCH), mybir.dt.float32, kind="ExternalOutput").ap()
    tables = [given.pop(f"tbl_{f}") for f in range(FIELDS)]
    build(nc, tables, *given.values(), y)
    got = run_bass_kernel_spmd(nc, [arrays], core_ids=[0])
    return got.results[0]["y"].reshape(BATCH, 1)
```

```python
from contextlib import ExitStack

import concourse.bass as bass
from concourse import mybir

FIELDS, DIM = 32, 64
PAIRS = FIELDS * (FIELDS - 1) // 2
PAIR_SPLIT = 4
PBLOCK = PAIRS // PAIR_SPLIT
BATCH, ROWS = 512, 128
TILES = BATCH // ROWS
STEPS = TILES // 2
D1, CTX, H1, H2 = 256, 16, 512, 256
GROUP = 4
GROUPS = FIELDS // GROUP
MIXED_FROM = 4
SPLIT_FIELDS = [j for j in range(FIELDS) if j // GROUP >= MIXED_FROM and j % GROUP >= GROUP // 2]
WHOLE_FIELDS = [j for j in range(1, FIELDS) if j not in SPLIT_FIELDS]
MIXED_GROUPS = GROUPS - MIXED_FROM
ACT_SHARE = 0.47
POOL_UNITS = (18, 21, 24, 27, 30, 33, 36, 39)
EARLY_GATHERS = 16
POOL_LEVELS = (32, 16, 8)
POOL_LAG = 5
KCHUNK = 16 * DIM
RAW_BUFFERS = 3


def first_column(j):
    return sum(k for k in WHOLE_FIELDS if k < j and k % 2 == j % 2) * DIM


def first_split_column(j):
    return sum(k for k in SPLIT_FIELDS if k < j) * DIM


KCOLS = max(first_column(j) + j * DIM for j in WHOLE_FIELDS)
KCHUNKS = -(-KCOLS // KCHUNK)
SPLIT_COLS = first_split_column(FIELDS)
JOINED = {1: 3, 4: 2}


def cut_units():
    order = []
    for group in range(GROUPS):
        kinds = [], []
        for j in range(max(1, group * GROUP), (group + 1) * GROUP):
            if any(first < j < first + fields for first, fields in JOINED.items()):
                continue
            if j in JOINED:
                kinds[0].append((j, 0, sum(range(j, j + JOINED[j]))))
                continue
            parts = 1 if j <= 16 else 2 if j < FIELDS - 2 else 3
            edges = [j * c // parts for c in range(parts + 1)]
            kinds[j in SPLIT_FIELDS].extend((j, a, b - a) for a, b in zip(edges, edges[1:]))
        for c in range(max(map(len, kinds))):
            order += [kind[c] for kind in kinds if c < len(kind)]
    return order


def segments(u):
    j, i0, left = UNITS_OF[u]
    at = 0
    while left:
        n = min(left, j - i0)
        yield j, i0, at, n
        j, i0, at, left = j + 1, 0, at + n, left - n


UNITS_OF = cut_units()
UNITS = len(UNITS_OF)
SEED = 2 * UNITS
T_BUFFERS = 3
PRODUCT_BUFFERS = 9
assert UNITS % T_BUFFERS == 0 and UNITS % PRODUCT_BUFFERS == 0
TAIL_STAGES = 5
TAIL_PARTS = {11: (0, 0, 4), 16: (1, 0, 1), 17: (1, 1, 2), 21: (2, 0, 1), 22: (2, 1, 2), 24: (2, 2, 3),
              25: (2, 3, 4), 31: (3, 0, 1), 32: (3, 1, 2), 37: (4, 0, 1)}
TAIL_BLOCKS = (PAIR_SPLIT, D1 // 128, H1 // 128, H2 // 128, 1)
LAST_PIJ_AT = 42
LAST_PIJ_BLOCKS = PAIR_SPLIT - 1


def act_pairs(u):
    if u in POOL_UNITS:
        return 0
    pairs = [0 if v in POOL_UNITS else UNITS_OF[v][2] for v in range(u + 1)]
    share = round(sum(pairs) * ACT_SHARE) - round(sum(pairs[:u]) * ACT_SHARE)
    return min(max(1, share), max(1, UNITS_OF[u][2] - 1))


def sums_behind(u):
    own = [u - 1] if u > 0 and u - 1 not in POOL_UNITS else []
    pooled = [u - POOL_LAG] if u - POOL_LAG in POOL_UNITS else []
    return own + pooled + ([u] if u == UNITS - 1 else [])


DVE_ORDER = [v for u in range(UNITS) for v in sums_behind(u)]
ACT_ORDER = [u for u in range(UNITS) if u not in POOL_UNITS]
assert sorted(DVE_ORDER) == list(range(UNITS)) and POOL_LAG < PRODUCT_BUFFERS


def summed(order, u):
    if u < 0:
        return summed(order, u + UNITS) - len(order)
    while u >= 0 and u not in order:
        u -= 1
    return order.index(u) + 1 if u >= 0 else 0


ROWS_AT = {0: 3, 3: 4, 11: 5, 18: 6, 26: 7, 34: 0, 37: 1, 40: 2}
FIRST_ROWS_AT = {0: 1, 1: 2, 4: 3, 6: 4, 13: 5, 19: 6, 26: 7, 34: 0, 37: 1, 40: 2}
NEXT_TILE_FROM = 34
ROWS_LAG = 2
ROW_SLOTS = 4


def in_last_pij(v):
    j, i0, _ = UNITS_OF[v]
    return j * (j - 1) // 2 + i0 < LAST_PIJ_BLOCKS * PBLOCK


def begins_group(u):
    group = UNITS_OF[u][0] // GROUP
    return group if u == 0 or UNITS_OF[u - 1][0] // GROUP != group else None


def in_slot(group):
    return [g for g in range(MIXED_FROM, GROUPS) if g % 2 == group % 2]


def rows_at(eng, step, h, u, do, lag=0):
    group, first = ROWS_AT.get(u - lag), FIRST_ROWS_AT.get(u - lag)
    if h == 0 and group != first:
        if first is not None:
            with eng.If(step < 1):
                do(step, h, first)
        if group is not None:
            with eng.If(step > 0):
                do(step, h, group)
    elif group is not None and u - lag < NEXT_TILE_FROM:
        do(step, h, group)
    elif group is not None and h == 0:
        do(step, 1, group)
    elif group is not None:
        with eng.If(step < STEPS - 1):
            do(step + 1, 0, group)


def units_through(group):
    if group < 0:
        return units_through(group + GROUPS) - UNITS
    return sum(j // GROUP <= group for j, *_ in UNITS_OF)


SPLIT_AHEAD = 4
SPLIT_LAG = 1
SPLIT_AT = dict(zip((0, 2, 5, 8), SPLIT_FIELDS[SPLIT_AHEAD:]))


def build(nc, tables, ids, k_cols, k_twice, w_pairs, b_pairs, ctx_t, w1, b1, w2, b2, w3, y):
    f32, f32r, i32 = mybir.dt.float32, mybir.dt.float32r, mybir.dt.int32
    ALU, ACT, AX = mybir.AluOpType, mybir.ActivationFunctionType, mybir.AxisListType

    ctx = ExitStack()
    with ctx:
        def sb(name, shape, dt=f32):
            return ctx.enter_context(nc.sbuf_tensor(name, shape, dt))

        def sem(name):
            return ctx.enter_context(nc.semaphore(name))

        k_sb = sb("k_sb", [128, KCOLS])
        ids_sb = sb("ids_sb", [ROWS, TILES + 1, FIELDS], i32)
        rows_id = [sb(f"rows_id{h}", [ROWS, FIELDS], i32) for h in range(2)]
        emb = [sb(f"emb{h}", [ROWS, FIELDS * DIM]) for h in range(2)]
        emb_t = [[sb(f"emb_t{s}{p}", [128, GROUP // 2 * ROWS]) for p in range(2)] for s in range(ROW_SLOTS)]
        emb_parts = [[sb(f"emb_parts{s}{p}", [128, 2, ROWS], f32r) for p in range(2)] for s in range(2)]
        k_raw = [sb(f"k_raw{r}", [128, (FIELDS - 1) * DIM]) for r in range(RAW_BUFFERS)]
        k_split = sb("k_split", [128, SPLIT_COLS], f32r)
        product = [sb(f"product{g}", [ROWS, 16, DIM]) for g in range(PRODUCT_BUFFERS)]
        pij = [sb(f"pij{h}", [ROWS, PAIRS]) for h in range(2)]
        pij_t = sb("pij_t", [PBLOCK, PAIR_SPLIT, ROWS])
        z_t = sb("z_t", [128, D1 // 128, ROWS])
        h1_t = sb("h1_t", [128, H1 // 128, ROWS])
        h2_t = sb("h2_t", [128, H2 // 128, ROWS])
        y_row = sb("y_row", [1, ROWS + BATCH])
        ident = sb("ident", [128, 128])
        w_pairs_sb = sb("w_pairs_sb", [PBLOCK, PAIR_SPLIT, D1])
        b_pairs_sb = sb("b_pairs_sb", [128, D1 // 128])
        ctx_sb = sb("ctx_sb", [CTX, ROWS + BATCH])
        w1z_sb = sb("w1z_sb", [128, D1 // 128, H1])
        w1c_sb = sb("w1c_sb", [CTX, H1])
        b1_sb = sb("b1_sb", [128, H1 // 128])
        w2_sb = sb("w2_sb", [128, H1 // 128, H2])
        b2_sb = sb("b2_sb", [128, H2 // 128])
        w3_sb = sb("w3_sb", [128, H2 // 128])

        t_ps = [ctx.enter_context(nc.psum_tensor(f"t_ps{p}", [ROWS, 16, DIM], f32))
                for p in range(T_BUFFERS)]
        emb_ps = ctx.enter_context(nc.psum_tensor("emb_ps", [128, 512], f32))
        tail_ps = ctx.enter_context(nc.psum_tensor("tail_ps", [128, 512], f32))

        ids_loaded = sem("ids_loaded")
        ids_copied = sem("ids_copied")
        gathered = [[sem(f"gathered{h}_{g}") for g in range(GROUPS)] for h in range(2)]
        k_loaded = [sem(f"k_loaded{c}") for c in range(KCHUNKS)]
        raw_loaded = [sem(f"raw_loaded{r}") for r in range(RAW_BUFFERS)]
        k_hi_ready = sem("k_hi_ready")
        k_split_ready = sem("k_split_ready")
        pool_added = sem("pool_added")
        weights_loaded = sem("weights_loaded")
        zeroed = sem("zeroed")
        ident_ready = sem("ident_ready")
        emb_in_psum = sem("emb_in_psum")
        emb_copied = sem("emb_copied")
        emb_split = sem("emb_split")
        rows_doubled = [sem(f"rows_doubled{s}") for s in range(2)]
        t_ready = sem("t_ready")
        product_ready = sem("product_ready")
        act_summed = sem("act_summed")
        dve_summed = sem("dve_summed")
        tail_mm = sem("tail_mm")
        tail_out = sem("tail_out")
        last_mm = sem("last_mm")
        last_act = sem("last_act")
        last_dve = sem("last_dve")
        y_stored = sem("y_stored")
        gathers_begun = sem("gathers_begun")

        WEIGHTS = [(w_pairs_sb[:, :, :], w_pairs), (b_pairs_sb[:, :], b_pairs),
                   (w1z_sb[:, :, :], w1[0:D1, :].rearrange("(c p) o -> p c o", p=128)),
                   (ctx_sb[:, :], ctx_t), (w1c_sb[:, :], w1[D1:D1 + CTX, :]), (b1_sb[:, :], b1),
                   (w2_sb[:, :, :], w2.rearrange("(c p) o -> p c o", p=128)),
                   (b2_sb[:, :], b2), (w3_sb[:, :], w3)]

        banks = [emb_ps[:, 0:ROWS]]
        banks += [t_ps[c // 2][:, c % 2 * 8:c % 2 * 8 + ROWS // DIM, :].rearrange("p a e -> p (a e)") for c in range(6)]
        banks += [tail_ps[:, 0:ROWS]]
        z_ps, h1_ps, h2_ps = banks[0:2], banks[2:6], banks[6:8]
        assert len(z_ps) == D1 // 128 and len(h1_ps) == H1 // 128 and len(h2_ps) == H2 // 128

        block = ctx.enter_context(nc.Block())

        @block.sync
        def _(sp):
            sp.dma_start(ids_sb[:, 0:TILES, :], ids.rearrange("(t b) f -> b t f", b=ROWS)).then_inc(ids_loaded, 16)
            for c in range(KCHUNKS):
                if c >= 1:
                    sp.wait_ge(gathered[0][min(c - 1, GROUPS // 2)], 16 * GROUP)
                cols = slice(c * KCHUNK, min((c + 1) * KCHUNK, KCOLS))
                sp.dma_start(k_sb[:, cols], k_cols[:, cols]).then_inc(k_loaded[c], 16)
            with sp.Fori(0, STEPS) as step:
                for h in range(2):
                    for c in range(MIXED_GROUPS):
                        slot = (MIXED_FROM + c) % 2
                        sp.wait_ge(emb_split, SEED + (step * 2 + h) * MIXED_GROUPS + c + 1)
                        for p in range(2):
                            own, other = slice(p * DIM, (p + 1) * DIM), slice((1 - p) * DIM, (2 - p) * DIM)
                            parts = emb_parts[slot][p]
                            sp.dma_start(parts[other, :, :].bitcast(f32), parts[own, :, :].bitcast(f32))\
                              .then_inc(rows_doubled[slot], 16)
                        if h == 0 and c == 0:
                            with sp.If(step < 1):
                                for to, of in WEIGHTS:
                                    sp.dma_start(to, of).then_inc(weights_loaded, 16)
            sp.wait_ge(last_act, 7)
            sp.dma_start(y, y_row[:, ROWS:ROWS + BATCH]).then_inc(y_stored, 16)
            sp.wait_ge(y_stored, 16)

        @block.gpsimd
        def _(pool):
            pool.memset(ident[:, :], 0.0).then_inc(ident_ready, 1)
            pool.wait_ge(ident_ready, 1)
            pool.affine_select(out=ident[:, :], in_=ident[:, :], compare_op=ALU.not_equal, fill=1.0,
                               base=0, pattern=[[-1, 128]], channel_multiplier=1).then_inc(ident_ready, 1)
            pool.wait_ge(ids_loaded, 16)

            def begin_gathers(step, h):
                pool.wait_ge(product_ready, SEED + (step * 2 + h - 1) * UNITS)
                pool.tensor_copy(rows_id[h][:, :], ids_sb[:, bass.ds(step * 2 + h, 1), :]
                                 if not isinstance(step, int) else ids_sb[:, step * 2 + h, :])\
                    .then_inc(ids_copied, 1)
                pool.wait_ge(ids_copied, step * 2 + h + 1)
                pool.sem_inc(gathers_begun, 1)

            def gather(h, fields):
                for f in fields:
                    pool.indirect_dma_start(
                        emb[h][:, f * DIM:(f + 1) * DIM], None, tables[f],
                        bass.IndirectOffsetOnAxis(rows_id[h][:, f:f + 1], 0),
                    ).then_inc(gathered[h][f // GROUP], 16)

            def add_products(step, h, u):
                tile, n = step * 2 + h, UNITS_OF[u][2]
                pool.wait_ge(product_ready, SEED + tile * UNITS + u + 1)
                for c, left in enumerate(POOL_LEVELS):
                    begun = (tile * len(POOL_UNITS) + POOL_UNITS.index(u)) * len(POOL_LEVELS) + c
                    terms = product[u % PRODUCT_BUFFERS]
                    if c > 0:
                        pool.wait_ge(pool_added, begun)
                    pool.tensor_tensor(terms[:, 0:n, 0:left], terms[:, 0:n, 0:left],
                                       terms[:, 0:n, left:2 * left], ALU.add).then_inc(pool_added, 1)

            def gather_next(step, h, fields):
                if h == 0:
                    gather(1, fields)
                else:
                    with pool.If(step < STEPS - 1):
                        gather(0, fields)

            begin_gathers(0, 0)
            gather(0, range(FIELDS))
            with pool.Fori(0, STEPS) as step:
                for h in range(2):
                    if h == 0:
                        begin_gathers(step, 1)
                    else:
                        with pool.If(step < STEPS - 1):
                            begin_gathers(step + 1, 0)
                    gather_next(step, h, range(EARLY_GATHERS))
                    each = (FIELDS - EARLY_GATHERS) // len(POOL_UNITS)
                    for c, u in enumerate(POOL_UNITS):
                        add_products(step, h, u)
                        gather_next(step, h, range(EARLY_GATHERS + c * each, EARLY_GATHERS + (c + 1) * each))

        @block.tensor
        def _(pe):
            pe.wait_ge(ident_ready, 2)
            pe.wait_ge(zeroed, 2 * ROW_SLOTS + 1)

            def transpose_rows(step, h, group):
                pe.wait_ge(emb_copied, SEED + (step * 2 + h) * GROUPS + group)
                splits = max(0, group - MIXED_FROM)
                pe.wait_ge(emb_split, SEED + (step * 2 + h) * MIXED_GROUPS + splits)
                pe.wait_ge(gathered[h][group], (step + 1) * 16 * GROUP)
                for m in range(GROUP // 2):
                    at = (group * GROUP + 2 * m) * DIM
                    done = pe.transpose(emb_ps[:, m * ROWS:(m + 1) * ROWS], emb[h][:, at:at + 2 * DIM], ident[:, :])
                done.then_inc(emb_in_psum, 1)

            def tail(tile, before, stage, first, end):
                if first == 0:
                    pe.wait_ge(tail_out, SEED + tile * TAIL_STAGES + stage)
                if stage == 0:
                    pe.wait_ge(dve_summed, SEED + tile * len(DVE_ORDER))
                    pe.wait_ge(act_summed, SEED + tile * len(ACT_ORDER))
                    for c in range(first, end):
                        done = pe.transpose(tail_ps[0:PBLOCK, c * ROWS:(c + 1) * ROWS],
                                            pij[before][:, c * PBLOCK:(c + 1) * PBLOCK], ident[:, :])
                if stage == 1:
                    pe.wait_ge(weights_loaded, 16 * len(WEIGHTS))
                    for o in range(first, end):
                        for c in range(PAIR_SPLIT):
                            done = pe.matmul(tail_ps[:, o * ROWS:(o + 1) * ROWS],
                                             w_pairs_sb[:, c, o * 128:(o + 1) * 128], pij_t[:, c, :],
                                             start=c == 0, stop=c == PAIR_SPLIT - 1)
                if stage == 2:
                    for o in range(first, end):
                        for c in range(D1 // 128):
                            pe.matmul(tail_ps[:, o * ROWS:(o + 1) * ROWS],
                                      w1z_sb[:, c, o * 128:(o + 1) * 128], z_t[:, c, :],
                                      start=c == 0, stop=False)
                        done = pe.matmul(tail_ps[:, o * ROWS:(o + 1) * ROWS],
                                         w1c_sb[:, o * 128:(o + 1) * 128],
                                         ctx_sb[:, bass.ds(tile * ROWS, ROWS)],
                                         start=False, stop=True)
                if stage == 3:
                    for o in range(first, end):
                        for c in range(H1 // 128):
                            done = pe.matmul(tail_ps[:, o * ROWS:(o + 1) * ROWS],
                                             w2_sb[:, c, o * 128:(o + 1) * 128], h1_t[:, c, :],
                                             start=c == 0, stop=c == H1 // 128 - 1)
                if stage == 4:
                    for c in range(H2 // 128):
                        done = pe.matmul(tail_ps[0:1, 0:ROWS], w3_sb[:, c:c + 1], h2_t[:, c, :],
                                         start=c == 0, stop=c == H2 // 128 - 1)
                if end == TAIL_BLOCKS[stage]:
                    done.then_inc(tail_mm, 1)

            transpose_rows(0, 0, 0)
            with pe.Fori(0, STEPS) as step:
                for h in range(2):
                    for u in range(UNITS):
                        rows_at(pe, step, h, u, transpose_rows)
                        group = begins_group(u)
                        if group is not None:
                            pe.wait_ge(emb_copied, SEED + (step * 2 + h) * GROUPS + group + 1)
                            if group >= MIXED_FROM:
                                slot = in_slot(group)
                                doubled = (step * 2 + h) * len(slot) + slot.index(group) + 1
                                pe.wait_ge(rows_doubled[group % 2], doubled * 32)
                        pe.wait_ge(product_ready, SEED + (step * 2 + h) * UNITS + u + 1 - T_BUFFERS)
                        for j, i0, first, n in segments(u):
                            edges = [first] + [b for b in (8,) if first < b < first + n] + [first + n]
                            parts = list(zip(edges, edges[1:]))
                            place = j % GROUP // 2
                            if j in WHOLE_FIELDS:
                                at = first_column(j) + i0 * DIM
                                for c in range(at // KCHUNK, (at + n * DIM - 1) // KCHUNK + 1):
                                    pe.wait_ge(k_loaded[c], 16)
                                for a, b in parts:
                                    cols = slice(at + (a - first) * DIM, at + (b - first) * DIM)
                                    rows = emb_t[j // GROUP % ROW_SLOTS][j % 2]
                                    done = pe.matmul(t_ps[u % T_BUFFERS][:, a:b, :],
                                                     rows[:, place * ROWS:(place + 1) * ROWS],
                                                     k_sb[:, cols], start=True, stop=True)
                            else:
                                at = first_split_column(j) + i0 * DIM
                                pe.wait_ge(k_split_ready, SPLIT_FIELDS.index(j) + 1)
                                for part in range(2):
                                    for a, b in parts:
                                        cols = slice(at + (a - first) * DIM, at + (b - first) * DIM)
                                        done = pe.matmul(t_ps[u % T_BUFFERS][:, a:b, :],
                                                         emb_parts[j // GROUP % 2][j % 2][:, part, :],
                                                         k_split[:, cols], start=part == 0, stop=part == 1)
                        done.then_inc(t_ready, 1)
                        if u in TAIL_PARTS:
                            tail(step * 2 + h, 1 - h, *TAIL_PARTS[u])

            pe.wait_ge(tail_out, SEED + TILES * TAIL_STAGES)
            early = [max(c for c, v in enumerate(order) if in_last_pij(v)) + 1 for order in (DVE_ORDER, ACT_ORDER)]
            pe.wait_ge(dve_summed, SEED + (TILES - 1) * len(DVE_ORDER) + early[0])
            pe.wait_ge(act_summed, SEED + (TILES - 1) * len(ACT_ORDER) + early[1])

            def transpose_pij(c):
                return pe.transpose(tail_ps[0:PBLOCK, c * ROWS:(c + 1) * ROWS],
                                    pij[1][:, c * PBLOCK:(c + 1) * PBLOCK], ident[:, :])

            def add_z(c):
                for o in range(D1 // 128):
                    done = pe.matmul(z_ps[o], w_pairs_sb[:, c, o * 128:(o + 1) * 128],
                                     pij_t[:, c, :], start=c == 0, stop=c == PAIR_SPLIT - 1)
                return done

            for c in range(LAST_PIJ_BLOCKS):
                done = transpose_pij(c)
            done.then_inc(last_mm, 1)
            pe.wait_ge(last_act, 1)
            pe.wait_ge(product_ready, SEED + TILES * UNITS - T_BUFFERS + 1)
            for c in range(LAST_PIJ_BLOCKS):
                add_z(c)
            pe.wait_ge(dve_summed, SEED + TILES * len(DVE_ORDER))
            pe.wait_ge(act_summed, SEED + TILES * len(ACT_ORDER))
            transpose_pij(LAST_PIJ_BLOCKS).then_inc(last_mm, 1)
            pe.wait_ge(last_act, 2)
            add_z(LAST_PIJ_BLOCKS).then_inc(last_mm, 1)
            pe.wait_ge(product_ready, SEED + TILES * UNITS)
            for o in range(H1 // 128):
                pe.matmul(h1_ps[o], w1c_sb[:, o * 128:(o + 1) * 128], ctx_sb[:, TILES * ROWS:(TILES + 1) * ROWS],
                          start=True, stop=False)
            pe.wait_ge(last_act, 3)
            pe.wait_ge(last_dve, 1)
            for o in range(H1 // 128):
                for c in range(D1 // 128):
                    done = pe.matmul(h1_ps[o], w1z_sb[:, c, o * 128:(o + 1) * 128], z_t[:, c, :],
                                     start=False, stop=c == D1 // 128 - 1)
                done.then_inc(last_mm, 1)
            for c in range(H1 // 128):
                if c % 2 == 0:
                    pe.wait_ge(last_act, 4 + c // 2)
                else:
                    pe.wait_ge(last_dve, 2 + c // 2)
                for o in range(H2 // 128):
                    done = pe.matmul(h2_ps[o], w2_sb[:, c, o * 128:(o + 1) * 128], h1_t[:, c, :],
                                     start=c == 0, stop=c == H1 // 128 - 1)
            done.then_inc(last_mm, 1)
            for c in range(H2 // 128):
                if c % 2 == 0:
                    pe.wait_ge(last_act, 6)
                else:
                    pe.wait_ge(last_dve, 4)
                done = pe.matmul(emb_ps[0:1, 0:ROWS], w3_sb[:, c:c + 1], h2_t[:, c, :],
                                 start=c == 0, stop=c == H2 // 128 - 1)
            done.then_inc(last_mm, 1)

        @block.vector
        def _(dve):
            for s in range(ROW_SLOTS):
                for p in range(2):
                    dve.memset(emb_t[s][p][(1 - p) * DIM:(2 - p) * DIM, :], 0.0).then_inc(zeroed, 1)
            dve.memset(pij[1][:, :], 0.0).then_inc(zeroed, 1)

            def sum_products(step, h, u):
                j, i0, n = UNITS_OF[u]
                tile, n = step * 2 + h, n - act_pairs(u)
                terms = product[u % PRODUCT_BUFFERS][:, 0:n, :]
                if u in POOL_UNITS:
                    done = (tile * len(POOL_UNITS) + POOL_UNITS.index(u) + 1) * len(POOL_LEVELS)
                    dve.wait_ge(pool_added, done)
                    terms = product[u % PRODUCT_BUFFERS][:, 0:n, 0:POOL_LEVELS[-1]]
                dve.wait_ge(product_ready, SEED + tile * UNITS + u + 1)
                q = j * (j - 1) // 2 + i0
                dve.tensor_reduce(pij[h][:, q:q + n], terms, AX.X, ALU.add).then_inc(dve_summed, 1)

            def split_kernel(j):
                c, at = SPLIT_FIELDS.index(j), first_split_column(j)
                dve.wait_ge(k_hi_ready, c + 1)
                low = k_split[DIM:2 * DIM, at:at + j * DIM]
                dve.tensor_tensor(low, k_raw[c % RAW_BUFFERS][DIM:2 * DIM, 0:j * DIM],
                                  low.bitcast(f32), ALU.subtract).then_inc(k_split_ready, 1)

            def split_rows(step, h, group):
                if group < MIXED_FROM:
                    return
                dve.wait_ge(emb_copied, SEED + (step * 2 + h) * GROUPS + group + 1)
                for p in range(2):
                    parts, own = emb_parts[group % 2][p], slice(p * DIM, (p + 1) * DIM)
                    done = dve.tensor_tensor(parts[own, 1, :], emb_ps[own, ROWS:2 * ROWS],
                                             parts[own, 0, :].bitcast(f32), ALU.subtract)
                done.then_inc(emb_split, 1)

            for j in SPLIT_FIELDS[:SPLIT_AHEAD]:
                split_kernel(j)
            with dve.Fori(0, STEPS) as step:
                for h in range(2):
                    dve.wait_ge(tail_mm, SEED + (step * 2 + h - 1) * TAIL_STAGES + 1)
                    for u in range(UNITS):
                        tile, before = step * 2 + h, u - PRODUCT_BUFFERS
                        dve.wait_ge(t_ready, SEED + tile * UNITS + u + 1)
                        dve.wait_ge(act_summed, SEED + tile * len(ACT_ORDER) + summed(ACT_ORDER, before))
                        dve.wait_ge(dve_summed, SEED + tile * len(DVE_ORDER) + summed(DVE_ORDER, before))
                        for _, i0, a, n in segments(u):
                            done = dve.tensor_tensor(
                                product[u % PRODUCT_BUFFERS][:, a:a + n, :], t_ps[u % T_BUFFERS][:, a:a + n, :],
                                emb[h][:, i0 * DIM:(i0 + n) * DIM].rearrange("p (i e) -> p i e", e=DIM), ALU.mult)
                        done.then_inc(product_ready, 1)
                        if max(ats.get(u - ROWS_LAG, 0) for ats in (ROWS_AT, FIRST_ROWS_AT)) >= MIXED_FROM:
                            rows_at(dve, step, h, u, split_rows, ROWS_LAG)
                        for v in sums_behind(u):
                            sum_products(step, h, v)
                        if h == 0 and u - SPLIT_LAG in SPLIT_AT:
                            with dve.If(step < 1):
                                split_kernel(SPLIT_AT[u - SPLIT_LAG])

            dve.wait_ge(last_mm, 3)
            dve.wait_ge(weights_loaded, 16 * len(WEIGHTS))
            dve.tensor_scalar(z_t[:, 1, :], z_ps[1], b_pairs_sb[:, 1:2], None, ALU.add)\
               .then_inc(last_dve, 1)
            for c in range(1, H1 // 128, 2):
                dve.wait_ge(last_mm, 4 + c)
                dve.tensor_scalar(h1_t[:, c, :], h1_ps[c], b1_sb[:, c:c + 1], 0.0, ALU.add, ALU.max)\
                   .then_inc(last_dve, 1)
            dve.wait_ge(last_mm, 8)
            dve.tensor_scalar(h2_t[:, 1, :], h2_ps[1], b2_sb[:, 1:2], 0.0, ALU.add, ALU.max)\
               .then_inc(last_dve, 1)

        @block.scalar
        def _(act):
            def load_raw(c):
                at, cols = first_split_column(SPLIT_FIELDS[c]), SPLIT_FIELDS[c] * DIM
                act.dma_start(k_raw[c % RAW_BUFFERS][:, 0:cols], k_twice[:, at:at + cols])\
                   .then_inc(raw_loaded[c % RAW_BUFFERS], 16)

            for c in range(RAW_BUFFERS):
                load_raw(c)
            for s in (product_ready, act_summed, dve_summed, t_ready, emb_copied, emb_split, tail_mm, tail_out):
                act.nop().then_inc(s, SEED)

            def copy_rows(step, h, group):
                tile = step * 2 + h
                act.wait_ge(emb_in_psum, tile * GROUPS + group + 1)
                held = group - ROW_SLOTS
                if group >= MIXED_FROM:
                    slot = in_slot(group)
                    held = max(held, group - 2 if group != slot[0] else slot[-1] - GROUPS)
                act.wait_ge(t_ready, SEED + tile * UNITS + units_through(held))
                for p in range(2):
                    own = slice(p * DIM, (p + 1) * DIM)
                    wholes = ROWS if group >= MIXED_FROM else 2 * ROWS
                    done = act.copy(emb_t[group % ROW_SLOTS][p][own, 0:wholes], emb_ps[own, 0:wholes])
                    if group >= MIXED_FROM:
                        done = act.copy(emb_parts[group % 2][p][own, 0, :], emb_ps[own, ROWS:2 * ROWS])
                done.then_inc(emb_copied, 1)

            def split_kernel(j):
                c, at = SPLIT_FIELDS.index(j), first_split_column(j)
                act.wait_ge(raw_loaded[c % RAW_BUFFERS], 16 * (c // RAW_BUFFERS + 1))
                act.copy(k_split[:, at:at + j * DIM], k_raw[c % RAW_BUFFERS][:, 0:j * DIM]).then_inc(k_hi_ready, 1)
                if 1 <= c <= len(SPLIT_FIELDS) - RAW_BUFFERS:
                    act.wait_ge(k_split_ready, c)
                    load_raw(c + RAW_BUFFERS - 1)

            def sum_products(step, h, u):
                j, i0, n = UNITS_OF[u]
                act.wait_ge(product_ready, SEED + (step * 2 + h) * UNITS + u + 1)
                q = j * (j - 1) // 2 + i0
                for i in range(n - act_pairs(u), n):
                    terms = product[u % PRODUCT_BUFFERS][:, i, :]
                    done = act.activation(terms, terms, ACT.Copy, accum_out=pij[h][:, q + i:q + i + 1])
                done.then_inc(act_summed, 1)

            def tail(tile, stage):
                act.wait_ge(tail_mm, SEED + tile * TAIL_STAGES + stage + 1)
                if stage == 0:
                    done = act.copy(pij_t[:, :, :].rearrange("q c b -> q (c b)"), tail_ps[0:PBLOCK, :])
                if stage == 1:
                    act.wait_ge(weights_loaded, 16 * len(WEIGHTS))
                    for o in range(D1 // 128):
                        done = act.activation(z_t[:, o, :], tail_ps[:, o * ROWS:(o + 1) * ROWS],
                                              ACT.Identity, bias=b_pairs_sb[:, o:o + 1])
                if stage == 2:
                    for o in range(H1 // 128):
                        done = act.activation(h1_t[:, o, :], tail_ps[:, o * ROWS:(o + 1) * ROWS],
                                              ACT.Relu, bias=b1_sb[:, o:o + 1])
                if stage == 3:
                    for o in range(H2 // 128):
                        done = act.activation(h2_t[:, o, :], tail_ps[:, o * ROWS:(o + 1) * ROWS],
                                              ACT.Relu, bias=b2_sb[:, o:o + 1])
                if stage == 4:
                    done = act.copy(y_row[:, bass.ds(tile * ROWS, ROWS)] if not isinstance(tile, int) else
                                    y_row[:, tile * ROWS:(tile + 1) * ROWS], tail_ps[0:1, 0:ROWS])
                done.then_inc(tail_out, 1)

            for j in SPLIT_FIELDS[:SPLIT_AHEAD]:
                split_kernel(j)
            copy_rows(0, 0, 0)
            with act.Fori(0, STEPS) as step:
                for h in range(2):
                    for u in range(UNITS):
                        if h == 0 and u in SPLIT_AT:
                            with act.If(step < 1):
                                split_kernel(SPLIT_AT[u])
                        rows_at(act, step, h, u, copy_rows)
                        if h == 1 and u == LAST_PIJ_AT:
                            with act.If(step > STEPS - 2):
                                act.wait_ge(last_mm, 1)
                                act.copy(pij_t[:, 0:LAST_PIJ_BLOCKS, :].rearrange("q c b -> q (c b)"),
                                         tail_ps[0:PBLOCK, 0:LAST_PIJ_BLOCKS * ROWS]).then_inc(last_act, 1)
                        if u not in POOL_UNITS:
                            sum_products(step, h, u)
                        if u in TAIL_PARTS:
                            stage, _, end = TAIL_PARTS[u]
                            if end == TAIL_BLOCKS[stage]:
                                tail(step * 2 + h, stage)
            act.wait_ge(last_mm, 2)
            act.copy(pij_t[:, LAST_PIJ_BLOCKS, :], tail_ps[0:PBLOCK, LAST_PIJ_BLOCKS * ROWS:]).then_inc(last_act, 1)
            act.wait_ge(last_mm, 3)
            act.activation(z_t[:, 0, :], z_ps[0], ACT.Identity, bias=b_pairs_sb[:, 0:1])\
               .then_inc(last_act, 1)
            for c in range(0, H1 // 128, 2):
                act.wait_ge(last_mm, 4 + c)
                act.activation(h1_t[:, c, :], h1_ps[c], ACT.Relu, bias=b1_sb[:, c:c + 1]).then_inc(last_act, 1)
            act.wait_ge(last_mm, 8)
            act.activation(h2_t[:, 0, :], h2_ps[0], ACT.Relu, bias=b2_sb[:, 0:1]).then_inc(last_act, 1)
            act.wait_ge(last_mm, 9)
            act.copy(y_row[:, TILES * ROWS:], emb_ps[0:1, 0:ROWS]).then_inc(last_act, 1)


def kernel(dense_ctx, ids, W_top1, b_top1, W_top2, b_top2, W_top3, L0_rec_kernel, L0_rec_W, L0_rec_b,
           **tbl):
    import numpy as np
    import concourse.bacc as bacc
    from concourse.bass_utils import run_bass_kernel_spmd

    def columns(v):
        return np.ascontiguousarray(np.asarray(v).reshape(-1, 128).T)

    i, j = np.triu_indices(FIELDS, k=1)
    number = {(int(a), int(b)): p for p, (a, b) in enumerate(zip(i, j))}
    order = [number[a, b] for b in range(FIELDS) for a in range(b)]
    kern = np.asarray(L0_rec_kernel)[:, order, :].reshape(DIM, PAIRS * DIM)
    k_cols = np.zeros((128, KCOLS), kern.dtype)
    for f in WHOLE_FIELDS:
        at, q, half = first_column(f), f * (f - 1) // 2 * DIM, f % 2 * DIM
        k_cols[half:half + DIM, at:at + f * DIM] = kern[:, q:q + f * DIM]
    split = [kern[:, f * (f - 1) // 2 * DIM:f * (f + 1) // 2 * DIM] for f in SPLIT_FIELDS]
    k_twice = np.concatenate([np.concatenate(split, axis=1)] * 2)
    w_pairs = np.asarray(L0_rec_W)[:, order].T.reshape(PAIR_SPLIT, PBLOCK, D1).transpose(1, 0, 2)

    ctx_t = np.zeros((CTX, ROWS + BATCH), np.asarray(dense_ctx).dtype)
    ctx_t[:, ROWS:] = np.asarray(dense_ctx).T

    arrays = {f"tbl_{f}": np.asarray(tbl[f"tbl_{f}"]) for f in range(FIELDS)}
    arrays |= {
        "ids": np.asarray(ids), "k_cols": k_cols, "k_twice": k_twice, "w_pairs": np.ascontiguousarray(w_pairs),
        "b_pairs": columns(L0_rec_b), "ctx_t": ctx_t,
        "w1": np.asarray(W_top1), "b1": columns(b_top1), "w2": np.asarray(W_top2),
        "b2": columns(b_top2), "w3": columns(W_top3),
    }
    nc = bacc.Bacc("TRN2", target_bir_lowering=False, num_devices=1)
    given = {name: nc.dram_tensor(name, a.shape, mybir.dt.from_np(a.dtype), kind="ExternalInput").ap()
             for name, a in arrays.items()}
    y = nc.dram_tensor("y", (1, BATCH), mybir.dt.float32, kind="ExternalOutput").ap()
    tables = [given.pop(f"tbl_{f}") for f in range(FIELDS)]
    build(nc, tables, *given.values(), y)
    got = run_bass_kernel_spmd(nc, [arrays], core_ids=[0])
    return got.results[0]["y"].reshape(BATCH, 1)
```
